# Optimizing a Trainium2 kernel written in Bass

```python
import numpy as np
import jax
import jax.numpy as jnp

def _softmax(x, axis=-1):
    return jax.nn.softmax(x, axis=axis)

def _gelu(x):
    return jax.nn.gelu(x, approximate=True)

def _silu(x):
    return jax.nn.silu(x)

def _sigmoid(x):
    return jax.nn.sigmoid(x)

def _layernorm(x, axis=-1, eps=1e-05):
    m = jnp.mean(x, axis=axis, keepdims=True)
    v = jnp.var(x, axis=axis, keepdims=True)
    return (x - m) / jnp.sqrt(v + eps)

def _scatter_add(tgt, idx, src, axis=0):
    return tgt.at[idx].add(src)

def _segment_sum(src, seg, n):
    return jax.ops.segment_sum(src, seg, n)
kernel_name = 'mk_adaln_attn_ffn_d1_seqx_r4_15242f'

def setup_inputs(seed: int=0):
    np.random.seed(seed)
    _w = jnp.asarray

    def _rec_inputs():
        import jax
        import jax.numpy as jnp
        _rk = jax.random.key(seed)
        x = -0.000125 + 0.9999 * jax.random.normal(jax.random.fold_in(_rk, 1), (128, 64, 1024), jnp.float32)
        _lenS = 64 - jax.random.randint(jax.random.fold_in(_rk, 7), (128,), 0, max(1, 64 // 4) + 1, jnp.int32)
        _lenS2 = 64 - jax.random.randint(jax.random.fold_in(_rk, 8), (128,), 0, max(1, 64 // 4) + 1, jnp.int32)
        cond_128 = 0.0061147 + 1.02565 * jax.random.normal(jax.random.fold_in(_rk, 11), (128, 128), jnp.float32)
        fside_S_0 = -0.022604 + 0.987366 * jax.random.normal(jax.random.fold_in(_rk, 12), (64,), jnp.float32)
        return (x, cond_128, fside_S_0)
    x, cond_128, fside_S_0 = _rec_inputs()

    def _L0_cond_setup():
        import jax, jax.numpy as jnp
        import numpy as np
        K = 8
        T = 1.0
        D_EMBD = 128
        IN_C = 64
        OUT_C = 64
        BS = 32
        H = 1024
        HID = 128
        key = jax.random.key(seed)
        ks = jax.random.split(key, 10)
        s = lambda fan_in: 1.0 / np.sqrt(fan_in)
        return {'x': jax.random.normal(ks[0], (BS, IN_C, H), dtype=jnp.float32), 'embedding': jax.random.normal(ks[1], (BS, D_EMBD), dtype=jnp.float32), 'W0': jax.random.normal(ks[2], (D_EMBD, HID), dtype=jnp.float32) * s(D_EMBD), 'b0': jnp.zeros((HID,), dtype=jnp.float32), 'W1': jax.random.normal(ks[3], (HID, HID), dtype=jnp.float32) * s(HID), 'b1': jnp.zeros((HID,), dtype=jnp.float32), 'W2': jax.random.normal(ks[4], (HID, K), dtype=jnp.float32) * s(HID), 'b2': jnp.zeros((K,), dtype=jnp.float32), 'weight': jax.random.normal(ks[5], (K, OUT_C, IN_C, 1), dtype=jnp.float32) * s(IN_C), 'bias_k': jax.random.normal(ks[6], (K, OUT_C), dtype=jnp.float32) * 0.1}
    _L0_cond_all = _L0_cond_setup()
    _L0_cond_in = {k: v for k, v in _L0_cond_all.items() if k in ('W0', 'b0', 'W1', 'b1', 'W2', 'b2', 'weight', 'bias_k')}
    del _L0_cond_all

    def _L0_attn_setup():
        import jax, jax.numpy as jnp
        import numpy as np
        B, S, HIDDEN = (2, 512, 1024)
        TP = 2
        PART = HIDDEN // TP
        NUM_HEADS = 16 // TP
        HEAD_DIM = PART // NUM_HEADS
        MASKED_BIAS = -10000.0
        key = jax.random.key(seed)
        k_x, k_wq, k_bq, k_wo, k_bo = jax.random.split(key, 5)
        x = jax.random.normal(k_x, (B, S, HIDDEN), dtype=jnp.float32)
        w_qkv = jax.random.normal(k_wq, (3 * PART, HIDDEN), dtype=jnp.float32) * 0.02
        b_qkv = jax.random.normal(k_bq, (3 * PART,), dtype=jnp.float32) * 0.02
        w_o = jax.random.normal(k_wo, (HIDDEN, PART), dtype=jnp.float32) * 0.02
        b_o = jax.random.normal(k_bo, (HIDDEN,), dtype=jnp.float32) * 0.02
        return {'x': x, 'w_qkv': w_qkv, 'b_qkv': b_qkv, 'w_o': w_o, 'b_o': b_o}
    _L0_attn_all = _L0_attn_setup()
    _L0_attn_in = {k: v for k, v in _L0_attn_all.items() if k in ('w_qkv', 'b_qkv', 'w_o', 'b_o')}
    del _L0_attn_all

    def _L0_cond2_setup():
        import jax, jax.numpy as jnp
        import numpy as np
        from jax import lax
        N, C_IN, L = (32, 64, 1024)
        C_OUT, K, GROUPS = (64, 9, 4)
        C_DIM, PAD, STRIDE = (128, 4, 1)
        key = jax.random.key(seed)
        k1, k2, k3, k4, k5 = jax.random.split(key, 5)
        x = jax.random.normal(k1, (N, C_IN, L), dtype=jnp.float32)
        c = jax.random.normal(k2, (N, C_DIM), dtype=jnp.float32)
        weight = jax.random.normal(k3, (C_OUT, C_IN // GROUPS, K), dtype=jnp.float32)
        c_weight = jax.random.normal(k4, (C_OUT, C_DIM), dtype=jnp.float32)
        bias = jax.random.normal(k5, (C_OUT,), dtype=jnp.float32)
        return {'x': x, 'c': c, 'weight': weight, 'c_weight': c_weight, 'bias': bias}
    _L0_cond2_all = _L0_cond2_setup()
    _L0_cond2_in = {k: v for k, v in _L0_cond2_all.items() if k in ('weight', 'c_weight')}
    del _L0_cond2_all

    def _L0_ffn_setup():
        import jax, jax.numpy as jnp
        import numpy as np
        import math
        IN_DIM = 1024
        FEATURES = 1024
        BATCH, SEQ = (8, 512)
        key = jax.random.key(seed)
        kx, kk = jax.random.split(key)
        x = jax.random.normal(kx, (BATCH, SEQ, IN_DIM), dtype=jnp.float32)
        kernel = jax.random.randint(kk, (IN_DIM, FEATURES), 0, 2) > 0
        scale = jnp.asarray(1.0 / math.sqrt(IN_DIM), dtype=jnp.float32)
        return {'x': x, 'kernel': kernel, 'scale': scale}
    _L0_ffn_all = _L0_ffn_setup()
    _L0_ffn_in = {k: v for k, v in _L0_ffn_all.items() if k in ('kernel', 'scale')}
    del _L0_ffn_all
    return {'x': x, 'cond_128': cond_128, 'fside_S_0': fside_S_0, 'L0_cond_W0': _L0_cond_in['W0'], 'L0_cond_b0': _L0_cond_in['b0'], 'L0_cond_W1': _L0_cond_in['W1'], 'L0_cond_b1': _L0_cond_in['b1'], 'L0_cond_W2': _L0_cond_in['W2'], 'L0_cond_b2': _L0_cond_in['b2'], 'L0_cond_weight': _L0_cond_in['weight'], 'L0_cond_bias_k': _L0_cond_in['bias_k'], 'L0_attn_w_qkv': _L0_attn_in['w_qkv'], 'L0_attn_b_qkv': _L0_attn_in['b_qkv'], 'L0_attn_w_o': _L0_attn_in['w_o'], 'L0_attn_b_o': _L0_attn_in['b_o'], 'L0_cond2_weight': _L0_cond2_in['weight'], 'L0_cond2_c_weight': _L0_cond2_in['c_weight'], 'L0_ffn_kernel': _L0_ffn_in['kernel'], 'L0_ffn_scale': _L0_ffn_in['scale']}

def reference(x, cond_128, fside_S_0, L0_cond_W0, L0_cond_b0, L0_cond_W1, L0_cond_b1, L0_cond_W2, L0_cond_b2, L0_cond_weight, L0_cond_bias_k, L0_attn_w_qkv, L0_attn_b_qkv, L0_attn_w_o, L0_attn_b_o, L0_cond2_weight, L0_cond2_c_weight, L0_ffn_kernel, L0_ffn_scale):
    import jax
    import jax.numpy as jnp

    def _L0_cond_ref(x, embedding, W0, b0, W1, b1, W2, b2, weight, bias_k):
        import jax, jax.numpy as jnp
        import numpy as np
        K = 8
        T = 1.0
        D_EMBD = 128
        IN_C = 64
        OUT_C = 64
        BS = 32
        H = 1024
        HID = 128
        h = jax.nn.gelu(embedding @ W0 + b0, approximate=False)
        h = jax.nn.gelu(h @ W1 + b1, approximate=False)
        att = jax.nn.softmax((h @ W2 + b2) / T, axis=-1)
        agg_w = jnp.einsum('bk,koi->boi', att, weight[..., 0])
        agg_b = att @ bias_k
        out = jnp.einsum('boi,bih->boh', agg_w, x) + agg_b[:, :, None]
        return out

    def _L0_attn_ref(x, w_qkv, b_qkv, w_o, b_o):
        import jax, jax.numpy as jnp
        import numpy as np
        B, S, HIDDEN = (2, 512, 1024)
        TP = 2
        PART = HIDDEN // TP
        NUM_HEADS = 16 // TP
        HEAD_DIM = PART // NUM_HEADS
        MASKED_BIAS = -10000.0
        b, s, _ = x.shape
        qkv = x @ w_qkv.T + b_qkv
        q, k, v = jnp.split(qkv, 3, axis=-1)

        def to_heads(a):
            return a.reshape(b, s, NUM_HEADS, HEAD_DIM).transpose(0, 2, 1, 3)
        q, k, v = (to_heads(q), to_heads(k), to_heads(v))
        scores = jnp.einsum('bhfc,bhtc->bhft', k, q)
        causal = jnp.triu(jnp.ones((s, s), dtype=bool))
        scores = jnp.where(causal[None, None], scores, MASKED_BIAS)
        attn = jax.nn.softmax(scores, axis=-2)
        vals = jnp.einsum('bhft,bhfc->bhtc', attn, v)
        vals = vals.transpose(0, 2, 1, 3).reshape(b, s, PART)
        out = vals @ w_o.T + b_o
        return out

    def _L0_cond2_ref(x, c, weight, c_weight, bias):
        import jax, jax.numpy as jnp
        import numpy as np
        from jax import lax
        N, C_IN, L = (32, 64, 1024)
        C_OUT, K, GROUPS = (64, 9, 4)
        C_DIM, PAD, STRIDE = (128, 4, 1)
        out = lax.conv_general_dilated(x, weight, window_strides=(STRIDE,), padding=[(PAD, PAD)], dimension_numbers=('NCH', 'OIH', 'NCH'), feature_group_count=GROUPS)
        ctx = jnp.einsum('nd,od->no', c, c_weight)
        out = out + ctx[:, :, None] + bias[None, :, None]
        return out

    def _L0_ffn_ref(x, kernel, scale):
        import jax, jax.numpy as jnp
        import numpy as np
        import math
        IN_DIM = 1024
        FEATURES = 1024
        BATCH, SEQ = (8, 512)
        w = kernel.astype(x.dtype) * 2.0 - 1.0
        return scale * jnp.einsum('bsi,if->bsf', x, w)
    x = x + _L0_attn_ref(_L0_cond_ref(x, cond_128, L0_cond_W0, L0_cond_b0, L0_cond_W1, L0_cond_b1, L0_cond_W2, L0_cond_b2, L0_cond_weight, L0_cond_bias_k), L0_attn_w_qkv, L0_attn_b_qkv, L0_attn_w_o, L0_attn_b_o)
    x = x + _L0_ffn_ref(_L0_cond2_ref(x, cond_128, L0_cond2_weight, L0_cond2_c_weight, fside_S_0), L0_ffn_kernel, L0_ffn_scale)
    return x

_drawn_inputs = setup_inputs


def setup_inputs(seed=0):
    import zlib

    import numpy as np

    out = dict(_drawn_inputs(seed))
    spreads = {'L0_cond_b0': (0.0, 0.8), 'L0_cond_b1': (0.0, 2.0), 'L0_cond_b2': (0.0, 2.0)}
    factors = {'L0_cond_W0': 6.548,
     'L0_cond_W1': 6.103,
     'L0_cond_W2': 5.842,
     'L0_cond_bias_k': 8.0,
     'L0_attn_b_qkv': 8.0,
     'L0_attn_b_o': 4.034}
    for name, (base, spread) in spreads.items():
        noise = np.random.default_rng([zlib.crc32(name.encode()), seed]).standard_normal(out[name].shape)
        drawn = base * np.exp(spread * noise) if base else spread * noise
        out[name] = jnp.asarray(drawn.astype(out[name].dtype))
    for name, factor in factors.items():
        out[name] = (out[name] * factor).astype(out[name].dtype)
    return out
```

```python
from contextlib import ExitStack

import numpy as np

import concourse.bass as bass
from concourse import mybir

F32 = mybir.dt.float32
F32R = mybir.dt.float32r
U8 = mybir.dt.uint8
ALU = mybir.AluOpType
ACT = mybir.ActivationFunctionType
AX = mybir.AxisListType

P = 128
BATCH, SEQ, HID = 128, 64, 1024
PAIRS = BATCH // 2
HC = HID // P
HEADS, HEAD = 8, 64
PART = HEADS * HEAD
HP = HEADS // 2
QKV = 3 * PART
EXPERTS = 8
TAPS, PAD = 9, 4
GROUPS = 4
GC = SEQ // GROUPS
PH = P // GC
NJ = HID // PH
BG = 2 * GROUPS
BANK = 512
MASKED = -10000.0


def live(t):
    return not isinstance(t, int) or 0 <= t < PAIRS


def at(r, c, d):
    r2, c2 = r + (c + d) // 2, (c + d) % 2
    return 2 * r2 + c2, r2, c2


def run_steps(eng, step, first, loop_from, loop_to, last):
    for s in range(first, loop_from):
        step(s // 2, s % 2)
    with eng.Fori(loop_from // 2, loop_to // 2) as r:
        step(r, 0)
        step(r, 1)
    for s in range(loop_to, last + 1):
        step(s // 2, s % 2)


def build(nc, x, cond, fside, w0, b0, w1, b1, w2, b2, experts, bias_k,
          w_qkv, b_qkv, w_o, b_o, conv_w, ctx_w, ffn_k, ffn_scale, out):
    x_rows = x.rearrange("(t b) i h -> t (b i) h", b=2)
    out_rows = out.rearrange("(t b) i h -> t (b i) h", b=2)

    mix_d = nc.dram_tensor("mix_d", [PAIRS, P, SEQ], F32, kind="Internal").ap()
    aggb_d = nc.dram_tensor("aggb_d", [PAIRS, 1, 2 * SEQ], F32, kind="Internal").ap()
    convb_d = nc.dram_tensor("convb_d", [PAIRS, 1, 2 * SEQ], F32, kind="Internal").ap()
    vals_d = nc.dram_tensor("vals_d", [PAIRS, P, HP * P], F32, kind="Internal").ap()
    x1_d = nc.dram_tensor("x1_d", [PAIRS, P, HID], F32, kind="Internal").ap()

    with ExitStack() as whole:
        ident = whole.enter_context(nc.sbuf_tensor("ident", [P, P], F32))
        with ExitStack() as phase:
            w_hi = phase.enter_context(nc.sbuf_tensor("w_hi", [P, HC, QKV], F32R))
            w_lo = phase.enter_context(nc.sbuf_tensor("w_lo", [P, HC, QKV], F32R))
            mask = phase.enter_context(nc.sbuf_tensor("mask", [P, SEQ], F32))
            masked = phase.enter_context(nc.sbuf_tensor("masked", [P, SEQ], F32))
            prepare(nc, cond, fside, w0, b0, w1, b1, w2, b2, experts, bias_k, ctx_w,
                    w_qkv, ident, mask, masked, w_hi, w_lo, mix_d, aggb_d, convb_d)
            attend(nc, x_rows, b_qkv, ident, mask, masked, w_hi, w_lo, mix_d, aggb_d, vals_d)
        feed_forward(nc, x_rows, w_o, b_o, conv_w, ffn_k, ffn_scale, ident,
                     convb_d, vals_d, x1_d, out_rows)


def prepare(nc, cond, fside, w0, b0, w1, b1, w2, b2, experts, bias_k, ctx_w,
            w_qkv, ident, mask, masked, w_hi, w_lo, mix_d, aggb_d, convb_d):
    FT = QKV // P
    WB = 4
    NB = 2 * FT
    OB = SEQ // 4
    with ExitStack() as ctx:
        def sb(name, shape, dt=F32):
            return ctx.enter_context(nc.sbuf_tensor(name, shape, dt))

        def sem(name):
            return ctx.enter_context(nc.semaphore(name))

        tri = sb("tri", [P, P])
        cond_sb = sb("cond_sb", [BATCH, P])
        w0_sb = sb("w0_sb", [P, P])
        w1_sb = sb("w1_sb", [P, P])
        w2_sb = sb("w2_sb", [P, EXPERTS])
        b0_sb = sb("b0_sb", [P, 1])
        b1_sb = sb("b1_sb", [P, 1])
        b2_sb = sb("b2_sb", [BATCH, EXPERTS])
        bk_sb = sb("bk_sb", [EXPERTS, SEQ])
        ctxw_sb = sb("ctxw_sb", [SEQ, P])
        fside_sb = sb("fside_sb", [BATCH, SEQ])
        exp_w = sb("exp_w", [EXPERTS, SEQ, 2, SEQ])
        w_rows = sb("w_rows", [P, WB, HID])
        cond_t = sb("cond_t", [P, BATCH])
        ctxw_t = sb("ctxw_t", [P, SEQ])
        h1 = sb("h1", [P, BATCH])
        h2 = sb("h2", [P, BATCH])
        logits = sb("logits", [BATCH, EXPERTS])
        neg_max = sb("neg_max", [BATCH, 1])
        att_sum = sb("att_sum", [BATCH, 1])
        att_inv = sb("att_inv", [BATCH, 1])
        att_e = sb("att_e", [BATCH, EXPERTS])
        att = sb("att", [BATCH, EXPERTS])
        att_t = sb("att_t", [EXPERTS, BATCH])
        aggb = sb("aggb", [BATCH, SEQ])
        convb = sb("convb", [BATCH, SEQ])
        mix = sb("mix", [P, PAIRS, SEQ])

        ps = [ctx.enter_context(nc.psum_tensor(f"prep{n}", [P, BANK], F32)) for n in range(8)]

        loaded, experts_in, rows_in = sem("loaded"), sem("experts_in"), [sem(f"rows_in{n}") for n in range(WB)]
        zeroed, consts = sem("zeroed"), sem("consts")
        masks = sem("masks")
        chain_pe, chain_act, chain_dve = sem("chain_pe"), sem("chain_act"), sem("chain_dve")
        mix_acc, mix_even, mix_odd = sem("mix_acc"), sem("mix_even"), sem("mix_odd")
        wt_acc, wt_hi, wt_lo = sem("wt_acc"), sem("wt_hi"), sem("wt_lo")
        stored = sem("stored")
        N_SMALL = 11

        with nc.Block() as block:
            @block.sync
            def _(sp):
                for dst, src in ((cond_sb[:, :], cond), (w0_sb[:, :], w0),
                                 (b0_sb[:, :], b0.rearrange("(p a) -> p a", a=1)), (w1_sb[:, :], w1),
                                 (b1_sb[:, :], b1.rearrange("(p a) -> p a", a=1)), (w2_sb[:, :], w2),
                                 (b2_sb[:, :], b2.rearrange("(a k) -> a k", a=1).to_broadcast([BATCH, EXPERTS])),
                                 (bk_sb[:, :], bias_k), (ctxw_sb[:, :], ctx_w),
                                 (fside_sb[:, :], fside.rearrange("(a k) -> a k", a=1).to_broadcast([BATCH, SEQ]))):
                    sp.dma_start(dst, src).then_inc(loaded, 16)
                for half in range(2):
                    sp.dma_start(exp_w[:, :, half, :], experts.rearrange("k o i a -> k o (i a)")).then_inc(experts_in, 16)
                for f in range(FT):
                    if f >= WB:
                        sp.wait_ge(wt_acc, 2 * (f - WB + 1))
                    sp.dma_start(w_rows[:, f % WB, :], w_qkv[f * P:(f + 1) * P, :]).then_inc(rows_in[f % WB], 16)
                    if f == WB:
                        sp.wait_ge(chain_dve, 9)
                        sp.dma_start(aggb_d.rearrange("t a (b o) -> (t a b) o", b=2), aggb[:, :]).then_inc(stored, 16)
                        sp.dma_start(convb_d.rearrange("t a (b o) -> (t a b) o", b=2), convb[:, :]).then_inc(stored, 16)
                sp.wait_ge(mix_even, OB)
                sp.wait_ge(mix_odd, OB)
                sp.dma_start(mix_d.rearrange("t p o -> p t o"), mix[:, :, :]).then_inc(stored, 16)
                sp.wait_ge(stored, 48)

            @block.gpsimd
            def _(pool):
                nc.gpsimd.memset(ident[:, :], 0.0).then_inc(zeroed, 1)
                nc.gpsimd.memset(tri[:, :], 1.0).then_inc(zeroed, 1)
                pool.wait_ge(zeroed, 2)
                nc.gpsimd.affine_select(out=ident[:, :], in_=ident[:, :], compare_op=ALU.not_equal, fill=1.0,
                                        base=0, pattern=[[-1, P]], channel_multiplier=1).then_inc(consts, 1)
                nc.gpsimd.affine_select(out=tri[:, :], in_=tri[:, :], compare_op=ALU.is_ge, fill=0.0,
                                        base=0, pattern=[[-1, P]], channel_multiplier=1).then_inc(consts, 1)

            @block.tensor
            def _(pe):
                pe.wait_ge(loaded, 160)
                pe.wait_ge(consts, 1)
                pe.transpose(ps[0][:, 0:BATCH], cond_sb[:, :], ident[:, :])
                pe.transpose(ps[0][:, P:P + SEQ], ctxw_sb[:, :], ident[0:SEQ, 0:SEQ]).then_inc(chain_pe, 1)
                pe.wait_ge(chain_dve, 2)
                pe.matmul(ps[1][:, 0:BATCH], w0_sb[:, :], cond_t[:, :], start=True, stop=True).then_inc(chain_pe, 1)
                pe.wait_ge(chain_act, 1)
                pe.matmul(ps[2][:, 0:BATCH], w1_sb[:, :], h1[:, :], start=True, stop=True).then_inc(chain_pe, 1)
                pe.wait_ge(chain_act, 2)
                pe.matmul(ps[3][:, 0:EXPERTS], h2[:, :], w2_sb[:, :], start=True, stop=True).then_inc(chain_pe, 1)
                pe.wait_ge(chain_dve, 6)
                pe.transpose(ps[1][0:EXPERTS, 0:BATCH], att[:, :], ident[:, :]).then_inc(chain_pe, 1)
                pe.wait_ge(chain_dve, 7)
                pe.matmul(ps[2][:, 0:SEQ], att_t[:, :], bk_sb[:, :], start=True, stop=True).then_inc(chain_pe, 1)
                pe.matmul(ps[3][:, 0:SEQ], cond_t[:, :], ctxw_t[:, :], start=True, stop=True).then_inc(chain_pe, 1)
                pe.wait_ge(experts_in, 32)
                for n in range(OB):
                    if n == 0:
                        pe.wait_ge(chain_dve, 9)
                    if n >= 4:
                        pe.wait_ge(mix_even, n - 3)
                        pe.wait_ge(mix_odd, n - 3)
                    for q in range(4):
                        last = pe.matmul(ps[n % 4][:, q * P:(q + 1) * P],
                                         exp_w[:, 4 * n + q, :, :].rearrange("k a i -> k (a i)"), att_t[:, :],
                                         start=True, stop=True)
                    last.then_inc(mix_acc, 1)
                for n in range(NB):
                    f, half = n // 2, n % 2
                    if half == 0:
                        pe.wait_ge(rows_in[f % WB], 16 * (f // WB + 1))
                    if n >= 4:
                        pe.wait_ge(wt_lo, n - 3)
                    for q in range(4):
                        h = 4 * half + q
                        last = pe.transpose(ps[4 + n % 4][:, q * P:(q + 1) * P],
                                            w_rows[:, f % WB, h * P:(h + 1) * P], ident[:, :])
                    last.then_inc(wt_acc, 1)

            def wt_out(w, n):
                f, half = n // 2, n % 2
                return w[:, 4 * half:4 * half + 4, f * P:(f + 1) * P]

            def mixed(n, parity):
                rows = slice(SEQ * parity, SEQ * parity + SEQ)
                return (mix[rows, :, 4 * n:4 * n + 4].rearrange("p t q -> p q t"),
                        ps[n % 4][rows, :].rearrange("p (q t b) -> p q t b", q=4, b=2)[:, :, :, parity])

            @block.scalar
            def _(act):
                act.wait_ge(chain_pe, 2)
                nc.scalar.activation(h1[:, :], ps[1][:, 0:BATCH], ACT.Gelu, bias=b0_sb[:, 0:1]).then_inc(chain_act, 1)
                act.wait_ge(chain_pe, 3)
                nc.scalar.activation(h2[:, :], ps[2][:, 0:BATCH], ACT.Gelu, bias=b1_sb[:, 0:1]).then_inc(chain_act, 1)
                act.wait_ge(chain_dve, 4)
                nc.scalar.activation(att_e[:, :], logits[:, :], ACT.Exp, bias=neg_max[:, 0:1],
                                     accum_out=att_sum[:, 0:1]).then_inc(chain_act, 1)
                for n in range(OB):
                    act.wait_ge(mix_acc, n + 1)
                    dst, src = mixed(n, 0)
                    nc.scalar.activation(dst, src, ACT.Copy).then_inc(mix_even, 1)
                for n in range(NB):
                    act.wait_ge(wt_acc, n + 1)
                    nc.scalar.activation(wt_out(w_hi, n), ps[4 + n % 4][:, :].rearrange("p (q f) -> p q f", q=4),
                                         ACT.Copy).then_inc(wt_hi, 1)

            @block.vector
            def _(dve):
                dve.wait_ge(consts, 2)
                for b in range(2):
                    rows = slice(SEQ * b, SEQ * b + SEQ)
                    last = nc.vector.tensor_copy(mask[rows, :], tri[rows, rows])
                last.then_inc(masks, 1)
                dve.wait_ge(masks, 1)
                nc.vector.tensor_scalar(masked[:, :], mask[:, :], -MASKED, MASKED, ALU.mult, ALU.add)
                dve.wait_ge(chain_pe, 1)
                nc.vector.tensor_copy(cond_t[:, :], ps[0][:, 0:BATCH]).then_inc(chain_dve, 1)
                nc.vector.tensor_copy(ctxw_t[:, :], ps[0][:, P:P + SEQ]).then_inc(chain_dve, 1)
                dve.wait_ge(chain_pe, 4)
                nc.vector.tensor_tensor(logits[:, :], ps[3][:, 0:EXPERTS], b2_sb[:, :], ALU.add).then_inc(chain_dve, 1)
                dve.wait_ge(chain_dve, 3)
                nc.vector.tensor_reduce(neg_max[:, :], logits[:, :], AX.X, ALU.max, negate=True).then_inc(chain_dve, 1)
                dve.wait_ge(chain_act, 3)
                nc.vector.reciprocal(att_inv[:, :], att_sum[:, :]).then_inc(chain_dve, 1)
                dve.wait_ge(chain_dve, 5)
                nc.vector.tensor_scalar(att[:, :], att_e[:, :], att_inv[:, 0:1], None, ALU.mult).then_inc(chain_dve, 1)
                dve.wait_ge(chain_pe, 5)
                nc.vector.tensor_copy(att_t[:, :], ps[1][0:EXPERTS, 0:BATCH]).then_inc(chain_dve, 1)
                dve.wait_ge(chain_pe, 7)
                nc.vector.tensor_copy(aggb[:, :], ps[2][:, 0:SEQ]).then_inc(chain_dve, 1)
                nc.vector.tensor_tensor(convb[:, :], ps[3][:, 0:SEQ], fside_sb[:, :], ALU.add).then_inc(chain_dve, 1)
                for n in range(OB):
                    dve.wait_ge(mix_even, n + 1)
                    dst, src = mixed(n, 1)
                    nc.vector.tensor_copy(dst, src).then_inc(mix_odd, 1)
                for n in range(NB):
                    dve.wait_ge(wt_hi, n + 1)
                    nc.vector.tensor_tensor(wt_out(w_lo, n), ps[4 + n % 4][:, :].rearrange("p (q f) -> p q f", q=4),
                                            wt_out(w_hi, n).bitcast(F32), ALU.subtract).then_inc(wt_lo, 1)


def attend(nc, x_rows, b_qkv, ident, mask, masked, w_hi, w_lo, mix_d, aggb_d, vals_d):
    with ExitStack() as ctx:
        def sb(name, shape, dt=F32):
            return ctx.enter_context(nc.sbuf_tensor(name, shape, dt))

        def bank(name):
            return ctx.enter_context(nc.psum_tensor(name, [P, BANK], F32))

        def sem(name):
            return ctx.enter_context(nc.semaphore(name))

        bias_sb = sb("bias_sb", [P, QKV])
        x_sb = sb("x_sb", [P, 2, HID])
        mix_sb = sb("mix_sb", [P, 2, P])
        aggb_sb = sb("aggb_sb", [P, 2, P])
        y_sum = sb("y_sum", [P, HC, P])
        y_hi = sb("y_hi", [P, 2, HC, P], F32R)
        y_lo = sb("y_lo", [P, 2, HC, P], F32R)
        qk = sb("qk", [P, 2, PART])
        v_sb = sb("v_sb", [P, 2, PART])
        qk_t = sb("qk_t", [P, 2, HP, P])
        scores = sb("scores", [P, HEADS, SEQ])
        row_max = sb("row_max", [P, HEADS])
        exps = sb("exps", [P, HEADS, SEQ])
        row_sum = sb("row_sum", [P, HEADS])
        row_inv = sb("row_inv", [P, HEADS])
        probs = sb("probs", [P, HEADS, P])
        probs_t = sb("probs_t", [P, HEADS, P])
        vals = sb("vals", [P, 2, HP, P])

        qkv_ps = [bank("qkv_ps0"), bank("qkv_ps1")]
        y_ps = [bank("y_ps0"), bank("y_ps1")]
        score_ps = [bank("score_ps0"), bank("score_ps1")]
        turn_ps = [bank("turn_ps0"), bank("turn_ps1")]

        inputs_in = [sem("inputs_in0"), sem("inputs_in1")]
        bias_in, cleared = sem("bias_in"), sem("cleared")
        y_acc, y_added, y_high, y_low = sem("y_acc"), sem("y_added"), sem("y_high"), sem("y_low")
        qkv_acc, qkv_out = sem("qkv_acc"), sem("qkv_out")
        turned, qk_t_out = sem("turned"), sem("qk_t_out")
        scores_acc, scores_cut, scores_masked = sem("scores_acc"), sem("scores_cut"), sem("scores_masked")
        maxed, shifted, exped, summed, inverted = (sem("maxed"), sem("shifted"), sem("exped"), sem("summed"),
                                                   sem("inverted"))
        probs_ready, probs_turned, probs_t_out = sem("probs_ready"), sem("probs_turned"), sem("probs_t_out")
        vals_acc, vals_out = sem("vals_acc"), sem("vals_out")
        vals_stored = [sem("vals_stored0"), sem("vals_stored1")]

        FIRST, LOOP, ENDS, LAST = -1, 4, PAIRS - 2, PAIRS + 1

        with nc.Block() as block:
            @block.sync
            def _(sp):
                sp.dma_start(bias_sb[:, :], b_qkv.rearrange("(a n) -> a n", a=1).to_broadcast([P, QKV])).then_inc(bias_in, 16)
                sp.wait_ge(cleared, 3)

                def load(t, r, c):
                    if live(t - 2):
                        sp.wait_ge(y_added, 2 * (t - 1))
                    sp.dma_start(x_sb[:, c, :], x_rows[t]).then_inc(inputs_in[c], 16)
                    for b in range(2):
                        half = slice(SEQ * b, SEQ * b + SEQ)
                        sp.dma_start(mix_sb[half, c, half], mix_d[t, half, :]).then_inc(inputs_in[c], 16)
                    sp.dma_start(aggb_sb[:, c, :], aggb_d[t].to_broadcast([P, P])).then_inc(inputs_in[c], 16)

                def store(t, r, c):
                    sp.wait_ge(vals_out, t + 1)
                    sp.dma_start(vals_d[t], vals[:, c, :, :].rearrange("p a n -> p (a n)")).then_inc(vals_stored[c], 16)

                def step(r, c):
                    if live(at(r, c, 2)[0]):
                        load(*at(r, c, 2))
                    if live(at(r, c, -2)[0]):
                        store(*at(r, c, -2))

                load(0, 0, 0)
                run_steps(sp, step, FIRST, LOOP, ENDS, LAST)
                for c in range(2):
                    sp.wait_ge(vals_stored[c], 16 * (PAIRS // 2))

            @block.gpsimd
            def _(pool):
                nc.gpsimd.memset(mix_sb[:, 0, :], 0.0).then_inc(cleared, 1)
                nc.gpsimd.memset(mix_sb[:, 1, :], 0.0).then_inc(cleared, 1)
                nc.gpsimd.memset(probs[:, :, :], 0.0).then_inc(cleared, 1)
                pool.wait_ge(cleared, 3)

                def add_masked(t, r, c):
                    pool.wait_ge(scores_cut, t + 1)
                    nc.gpsimd.tensor_tensor(scores[:, :, :], scores[:, :, :],
                                            masked[:, :].unsqueeze(1).to_broadcast([P, HEADS, SEQ]),
                                            ALU.add).then_inc(scores_masked, 1)

                def low_part(t, r, c):
                    for b in range(2):
                        chunks = slice(4 * b, 4 * b + 4)
                        pool.wait_ge(y_high, 2 * t + b + 1)
                        nc.gpsimd.tensor_tensor(y_lo[:, c, chunks, :], y_sum[:, chunks, :],
                                                y_hi[:, c, chunks, :].bitcast(F32), ALU.subtract).then_inc(y_low, 1)

                def step(r, c):
                    if live(at(r, c, -1)[0]):
                        add_masked(*at(r, c, -1))
                    if live(at(r, c, 1)[0]):
                        low_part(*at(r, c, 1))

                run_steps(pool, step, FIRST, LOOP, ENDS, LAST)

            @block.scalar
            def _(act):
                def values_out(t, r, c):
                    act.wait_ge(vals_acc, t + 1)
                    if live(t - 2):
                        act.wait_ge(vals_stored[c], 16 * r)
                    nc.scalar.activation(vals[:, c, :, :], turn_ps[0][:, :].rearrange("p (a n) -> p a n", a=HP),
                                         ACT.Copy).then_inc(vals_out, 1)

                def exponent(t, r, c):
                    act.wait_ge(shifted, t + 1)
                    if live(t - 1):
                        act.wait_ge(probs_ready, t)
                    nc.scalar.activation(exps[:, :, :], scores[:, :, :], ACT.Exp).then_inc(exped, 1)

                def high_part(t, r, c):
                    if live(t - 2):
                        act.wait_ge(qkv_acc, 3 * (t - 1))
                    for b in range(2):
                        chunks = slice(4 * b, 4 * b + 4)
                        act.wait_ge(y_added, 2 * t + b + 1)
                        nc.scalar.activation(y_hi[:, c, chunks, :], y_sum[:, chunks, :], ACT.Copy).then_inc(y_high, 1)

                def qk_turned_out(t, r, c):
                    if live(t - 1):
                        act.wait_ge(scores_acc, t)
                    for j in range(2):
                        act.wait_ge(turned, 2 * t + j + 1)
                        nc.scalar.activation(qk_t[:, j, :, :], turn_ps[j][:, :].rearrange("p (a n) -> p a n", a=HP),
                                             ACT.Copy).then_inc(qk_t_out, 1)

                def probs_turned_out(t, r, c):
                    if live(t - 1):
                        act.wait_ge(vals_acc, t)
                    for b in range(2):
                        act.wait_ge(probs_turned, 2 * t + b + 1)
                        nc.scalar.activation(probs_t[:, 4 * b:4 * b + 4, :],
                                             y_ps[b][:, :].rearrange("p (a n) -> p a n", a=4),
                                             ACT.Copy).then_inc(probs_t_out, 1)

                def step(r, c):
                    if live(at(r, c, -2)[0]):
                        values_out(*at(r, c, -2))
                    if live(at(r, c, -1)[0]):
                        exponent(*at(r, c, -1))
                    if live(at(r, c, 1)[0]):
                        high_part(*at(r, c, 1))
                    if live(at(r, c, 0)[0]):
                        qk_turned_out(*at(r, c, 0))
                    if live(at(r, c, -1)[0]):
                        probs_turned_out(*at(r, c, -1))

                run_steps(act, step, FIRST, LOOP, ENDS, LAST)

            @block.vector
            def _(dve):
                dve.wait_ge(bias_in, 16)

                def qkv_part_out(t, r, c, j):
                    dve.wait_ge(qkv_acc, 3 * t + j + 1)
                    if j < 2:
                        if live(t - 1):
                            dve.wait_ge(turned, 2 * t + j - 1)
                        dst = qk[:, j, :]
                    else:
                        if live(t - 2):
                            dve.wait_ge(vals_acc, t - 1)
                        dst = v_sb[:, c, :]
                    nc.vector.tensor_tensor(dst, qkv_ps[(c + j) % 2][:, :], bias_sb[:, j * PART:(j + 1) * PART],
                                            ALU.add).then_inc(qkv_out, 1)

                def softmax(t, r, c):
                    dve.wait_ge(scores_acc, t + 1)
                    if live(t - 1):
                        dve.wait_ge(exped, t)
                    for parity in range(2):
                        last = nc.vector.tensor_tensor(
                            scores[:, HP * parity:HP * parity + HP, :],
                            score_ps[parity][:, 0:HP * SEQ].rearrange("p (a f) -> p a f", a=HP),
                            mask[:, :].unsqueeze(1).to_broadcast([P, HP, SEQ]), ALU.mult)
                    last.then_inc(scores_cut, 1)
                    dve.wait_ge(scores_masked, t + 1)
                    nc.vector.tensor_reduce(row_max[:, :], scores[:, :, :], AX.X, ALU.max).then_inc(maxed, 1)
                    dve.wait_ge(maxed, t + 1)
                    nc.vector.tensor_tensor(scores[:, :, :], scores[:, :, :],
                                            row_max[:, :].unsqueeze(2).to_broadcast([P, HEADS, SEQ]),
                                            ALU.subtract).then_inc(shifted, 1)
                    dve.wait_ge(exped, t + 1)
                    nc.vector.tensor_reduce(row_sum[:, :], exps[:, :, :], AX.X, ALU.add).then_inc(summed, 1)
                    dve.wait_ge(summed, t + 1)
                    nc.vector.reciprocal(row_inv[:, :], row_sum[:, :]).then_inc(inverted, 1)

                def normalise(t, r, c):
                    dve.wait_ge(inverted, t + 1)
                    if live(t - 1):
                        dve.wait_ge(probs_turned, 2 * t)
                    for b in range(2):
                        half = slice(SEQ * b, SEQ * b + SEQ)
                        for parity in range(2):
                            heads = slice(HP * parity, HP * parity + HP)
                            last = nc.vector.tensor_tensor(
                                probs[half, :, half].rearrange("p (a e) f -> p e a f", e=2)[:, parity],
                                exps[half, heads, :],
                                row_inv[half, heads].unsqueeze(2).to_broadcast([SEQ, HP, SEQ]), ALU.mult)
                    last.then_inc(probs_ready, 1)

                def add_bias(t, r, c):
                    for b in range(2):
                        chunks = slice(4 * b, 4 * b + 4)
                        dve.wait_ge(y_acc, 2 * t + b + 1)
                        if live(t - 1):
                            dve.wait_ge(y_low, 2 * t + b - 1)
                        nc.vector.tensor_tensor(y_sum[:, chunks, :], y_ps[b][:, :].rearrange("p (a n) -> p a n", a=4),
                                                aggb_sb[:, c, :].unsqueeze(1).to_broadcast([P, 4, P]),
                                                ALU.add).then_inc(y_added, 1)

                def step(r, c):
                    t = at(r, c, 0)[0]
                    if live(t):
                        qkv_part_out(*at(r, c, 0), 0)
                    if live(at(r, c, -1)[0]):
                        softmax(*at(r, c, -1))
                        normalise(*at(r, c, -1))
                    if live(t):
                        qkv_part_out(*at(r, c, 0), 1)
                    if live(at(r, c, 1)[0]):
                        add_bias(*at(r, c, 1))
                    if live(t):
                        qkv_part_out(*at(r, c, 0), 2)

                run_steps(dve, step, FIRST, LOOP, ENDS, LAST)

            @block.tensor
            def _(pe):
                def mix_x(t, r, c):
                    pe.wait_ge(inputs_in[c], 64 * (r + 1))
                    if live(t - 3):
                        pe.wait_ge(probs_t_out, 2 * (t - 2))
                    for h in range(HC):
                        last = pe.matmul(y_ps[h // 4][:, (h % 4) * P:(h % 4 + 1) * P], x_sb[:, c, h * P:(h + 1) * P],
                                         mix_sb[:, c, :], start=True, stop=True)
                        if h % 4 == 3:
                            last.then_inc(y_acc, 1)

                def qkv_part(t, r, c, j):
                    if j == 0:
                        pe.wait_ge(y_low, 2 * (t + 1))
                    if not isinstance(t, int) or 3 * t + j >= 2:
                        pe.wait_ge(qkv_out, 3 * t + j - 1)
                    n = 0
                    for h in range(HC):
                        for y, w in ((y_hi, w_hi), (y_hi, w_lo), (y_lo, w_hi)):
                            last = pe.matmul(qkv_ps[(c + j) % 2][:, :], y[:, c, h, :], w[:, h, j * PART:(j + 1) * PART],
                                             start=(n == 0), stop=(n == 3 * HC - 1))
                            n += 1
                    last.then_inc(qkv_acc, 1)

                def turn_qk(t, r, c):
                    if live(t - 2):
                        pe.wait_ge(vals_out, t - 1)
                    for j in range(2):
                        pe.wait_ge(qkv_out, 3 * t + j + 1)
                        for a in range(HP):
                            last = pe.transpose(turn_ps[j][:, a * P:(a + 1) * P], qk[:, j, a * P:(a + 1) * P], ident[:, :])
                        last.then_inc(turned, 1)

                def score(t, r, c):
                    pe.wait_ge(qk_t_out, 2 * (t + 1))
                    if live(t - 1):
                        pe.wait_ge(scores_cut, t)
                    pe.nop(nofuse=True)
                    for a in range(HP):
                        for b in range(2):
                            rows = slice(SEQ * b, SEQ * b + SEQ)
                            for parity in range(2):
                                head = slice(HEAD * parity, HEAD * parity + HEAD)
                                last = pe.matmul(score_ps[parity][rows, a * SEQ:(a + 1) * SEQ],
                                                 qk_t[head, 0, a, rows], qk_t[head, 1, a, rows], start=True, stop=True)
                    last.then_inc(scores_acc, 1)

                def turn_probs(t, r, c):
                    pe.wait_ge(probs_ready, t + 1)
                    pe.wait_ge(y_added, min(2 * (t + 3), 2 * PAIRS) if isinstance(t, int) else 2 * (t + 3))
                    for head in range(HEADS):
                        last = pe.transpose(y_ps[head // 4][:, (head % 4) * P:(head % 4 + 1) * P], probs[:, head, :], ident[:, :])
                        if head % 4 == 3:
                            last.then_inc(probs_turned, 1)

                def values(t, r, c):
                    pe.wait_ge(probs_t_out, 2 * (t + 1))
                    if live(t + 1):
                        pe.wait_ge(qk_t_out, 2 * t + 3)
                    pe.nop(nofuse=True)
                    for a in range(HP):
                        for parity in range(2):
                            head = 2 * a + parity
                            last = pe.matmul(turn_ps[0][HEAD * parity:HEAD * parity + HEAD, a * P:(a + 1) * P],
                                             v_sb[:, c, head * HEAD:(head + 1) * HEAD], probs_t[:, head, :],
                                             start=True, stop=True)
                    last.then_inc(vals_acc, 1)

                def step(r, c):
                    t = at(r, c, 0)[0]
                    if live(t):
                        qkv_part(*at(r, c, 0), 0)
                    if live(at(r, c, -2)[0]):
                        values(*at(r, c, -2))
                    if live(at(r, c, -1)[0]):
                        score(*at(r, c, -1))
                    if live(t):
                        qkv_part(*at(r, c, 0), 1)
                    if live(at(r, c, 1)[0]):
                        mix_x(*at(r, c, 1))
                    if live(t):
                        qkv_part(*at(r, c, 0), 2)
                        turn_qk(*at(r, c, 0))
                    if live(at(r, c, -1)[0]):
                        turn_probs(*at(r, c, -1))

                run_steps(pe, step, FIRST, LOOP, ENDS, LAST)


def feed_forward(nc, x_rows, w_o, b_o, conv_w, ffn_k, ffn_scale, ident, convb_d, vals_d, x1_d, out_rows):
    CK = 24
    with ExitStack() as ctx:
        def sb(name, shape, dt=F32):
            return ctx.enter_context(nc.sbuf_tensor(name, shape, dt))

        def bank(name):
            return ctx.enter_context(nc.psum_tensor(name, [P, BANK], F32))

        def sem(name):
            return ctx.enter_context(nc.semaphore(name))

        wo_hi = sb("wo_hi", [P, HP, HID], F32R)
        wo_lo = sb("wo_lo", [P, HP, HID], F32R)
        signs = sb("signs", [P, PH, HID], F32R)
        band_hi = sb("band_hi", [P, 2, GROUPS, P], F32R)
        band_lo = sb("band_lo", [P, 2, GROUPS, P], F32R)
        scale_sb = sb("scale_sb", [P, 1])
        bo_sb = sb("bo_sb", [P, HID])

        out_ps = [bank("out_ps0"), bank("out_ps1")]
        ffn_ps = [bank("ffn_ps0"), bank("ffn_ps1")]
        conv_ps = [bank("conv_ps0"), bank("conv_ps1")]
        spare_ps = [bank("spare_ps0"), bank("spare_ps1")]

        with ExitStack() as prep:
            wo_rows = prep.enter_context(nc.sbuf_tensor("wo_rows", [P, PH, PART], F32))
            kernel_u8 = prep.enter_context(nc.sbuf_tensor("kernel_u8", [P, PH, HID], U8))
            conv_rows = prep.enter_context(nc.sbuf_tensor("conv_rows", [SEQ, GC, TAPS], F32))
            conv_pad = prep.enter_context(nc.sbuf_tensor("conv_pad", [SEQ, CK, GC], F32))
            wo_in, ffn_in, conv_in = sem("wo_in"), sem("ffn_in"), sem("conv_in")
            wo_turned, wo_high, wo_low = sem("wo_turned"), sem("wo_high"), sem("wo_low")
            pad_zero, padded = sem("pad_zero"), sem("padded")
            bands_turned, bands_high = sem("bands_turned"), sem("bands_high")
            wo_ps = out_ps + ffn_ps
            band_ps = conv_ps

            with nc.Block() as block:
                @block.sync
                def _(sp):
                    sp.dma_start(wo_rows[:, :, :], w_o.rearrange("(j p) n -> j p n", p=PH)).then_inc(wo_in, 16)
                    sp.dma_start(conv_rows[:, :, :], conv_w).then_inc(conv_in, 16)
                    sp.dma_start(kernel_u8[:, :, :], ffn_k.rearrange("(j p) f -> j p f", p=PH)).then_inc(ffn_in, 16)
                    sp.dma_start(scale_sb[:, :], ffn_scale.to_broadcast([P, 1])).then_inc(conv_in, 16)
                    sp.dma_start(bo_sb[:, :], b_o.rearrange("(a n) -> a n", a=1).to_broadcast([P, HID])).then_inc(conv_in, 16)
                    sp.wait_ge(conv_in, 48)

                @block.gpsimd
                def _(pool):
                    nc.gpsimd.memset(conv_pad[:, :, :], 0.0).then_inc(pad_zero, 1)
                    pool.wait_ge(ffn_in, 16)
                    for p in range(6, PH):
                        nc.gpsimd.tensor_scalar(signs[:, p, :], kernel_u8[:, p, :], 2.0, -1.0, ALU.mult, ALU.add)

                @block.tensor
                def _(pe):
                    pe.wait_ge(padded, 1)
                    for d in range(2):
                        for q in range(PH):
                            first = 7 + PH * d - q
                            last = pe.transpose(band_ps[d][:, q * SEQ:(q + 1) * SEQ],
                                                conv_pad[:, first:first + PH, :].rearrange("o k i -> o (k i)"),
                                                ident[0:SEQ, 0:SEQ])
                        last.then_inc(bands_turned, 1)
                    pe.wait_ge(wo_in, 16)
                    for p in range(PH):
                        if p >= 4:
                            pe.wait_ge(wo_low, p - 3)
                        for a in range(HP):
                            last = pe.transpose(wo_ps[p % 4][:, a * P:(a + 1) * P], wo_rows[:, p, a * P:(a + 1) * P], ident[:, :])
                        last.then_inc(wo_turned, 1)

                def band(m, d):
                    return m[:, d, :, :].rearrange("p g (q o) -> p q g o", q=PH)

                def band_src(d, q):
                    return band_ps[d][:, q * SEQ:(q + 1) * SEQ].rearrange("p (g o) -> p g o", g=GROUPS)

                @block.scalar
                def _(act):
                    for d in range(2):
                        act.wait_ge(bands_turned, d + 1)
                        for q in range(PH):
                            last = nc.scalar.activation(band(band_hi, d)[:, q], band_src(d, q), ACT.Copy)
                        last.then_inc(bands_high, 1)
                    for p in range(PH):
                        act.wait_ge(wo_turned, p + 1)
                        nc.scalar.activation(wo_hi[:, :, p * P:(p + 1) * P],
                                             wo_ps[p % 4][:, :].rearrange("p (a n) -> p a n", a=HP),
                                             ACT.Copy).then_inc(wo_high, 1)
                    act.wait_ge(ffn_in, 16)
                    for p in range(3, 6):
                        nc.scalar.activation(signs[:, p, :], kernel_u8[:, p, :], ACT.Copy, scale=2.0, bias=-1.0)

                @block.vector
                def _(dve):
                    dve.wait_ge(conv_in, 48)
                    dve.wait_ge(pad_zero, 1)
                    nc.vector.tensor_copy(conv_pad[:, 7:7 + TAPS, :], conv_rows[:, :, :].rearrange("o i k -> o k i")).then_inc(padded, 1)
                    for d in range(2):
                        dve.wait_ge(bands_high, d + 1)
                        for q in range(PH):
                            nc.vector.tensor_tensor(band(band_lo, d)[:, q], band_src(d, q),
                                                    band(band_hi, d)[:, q].bitcast(F32), ALU.subtract)
                    for p in range(PH):
                        dve.wait_ge(wo_high, p + 1)
                        nc.vector.tensor_tensor(wo_lo[:, :, p * P:(p + 1) * P],
                                                wo_ps[p % 4][:, :].rearrange("p (a n) -> p a n", a=HP),
                                                wo_hi[:, :, p * P:(p + 1) * P].bitcast(F32),
                                                ALU.subtract).then_inc(wo_low, 1)
                    dve.wait_ge(ffn_in, 16)
                    for p in range(3):
                        nc.vector.tensor_scalar(signs[:, p, :], kernel_u8[:, p, :], 2.0, -1.0, ALU.mult, ALU.add)

        vals = sb("vals_in", [P, 2, HP, P])
        vals_hi = sb("vals_hi", [P, 2, HP, P], F32R)
        vals_lo = sb("vals_lo", [P, 2, HP, P], F32R)
        x_sb = sb("x_res", [P, 2, HID])
        x1 = sb("x1", [P, 2, PH, NJ])
        x1_res = sb("x1_res", [P, 2, PH, NJ])
        win = sb("win", [P, 2, BG, NJ + 1])
        win_hi = sb("win_hi", [P, 2, BG, NJ + 1], F32R)
        win_lo = sb("win_lo", [P, 2, BG, NJ + 1], F32R)
        convb_sb = sb("convb_sb", [P, 2, BG, GC])
        conv = sb("conv", [P, PH, BG, GC])
        conv_hi = sb("conv_hi", [P, 2, PH, BG, GC], F32R)
        conv_lo = sb("conv_lo", [P, 2, PH, BG, GC], F32R)
        result = sb("result", [P, 2, HID])

        attn_in = [sem("attn_in0"), sem("attn_in1")]
        convb_in = [sem("convb_in0"), sem("convb_in1")]
        x1_stored = [sem("x1_stored0"), sem("x1_stored1")]
        win_in = [sem("win_in0"), sem("win_in1")]
        x1_in = [sem("x1_in0"), sem("x1_in1")]
        out_stored = [sem("out_stored0"), sem("out_stored1")]
        edges = sem("edges")
        vals_high, vals_low = sem("vals_high"), sem("vals_low")
        x_biased = sem("x_biased")
        out_acc, x1_ready = sem("out_acc"), sem("x1_ready")
        win_high, win_low = sem("win_high"), sem("win_low")
        conv_acc, conv_added, conv_high, conv_low = sem("conv_acc"), sem("conv_added"), sem("conv_high"), sem("conv_low")
        ffn_acc, result_ready = sem("ffn_acc"), sem("result_ready")

        FIRST, LOOP, ENDS, LAST = -3, 2, PAIRS - 4, PAIRS - 1
        H4 = PH // 2

        with nc.Block() as block:
            @block.sync
            def _(sp):
                def load_attention(t, r, c):
                    if live(t - 2):
                        sp.wait_ge(x1_ready, 2 * (t - 1))
                    sp.dma_start(vals[:, c, :, :].rearrange("p a n -> p (a n)"), vals_d[t]).then_inc(attn_in[c], 16)
                    sp.dma_start(x_sb[:, c, :], x_rows[t]).then_inc(attn_in[c], 16)

                def store_x1(t, r, c):
                    sp.wait_ge(x1_ready, 2 * (t + 1))
                    sp.dma_start(x1_d[t], x1[:, c, :, :].rearrange("p q j -> p (q j)")).then_inc(x1_stored[c], 16)

                def load_window(t, r, c):
                    if live(t - 2):
                        sp.wait_ge(conv_added, 2 * (t - 1))
                    sp.dma_start(convb_sb[:, c, :, :].rearrange("p g o -> p (g o)"),
                                 convb_d[t].to_broadcast([P, P])).then_inc(convb_in[c], 16)
                    sp.wait_ge(x1_stored[c], 16 * (r + 1))
                    if live(t - 2):
                        sp.wait_ge(win_low, t - 1)
                    phases = x1_d[t].rearrange("(g i) (p j) -> p i g j", i=GC, p=PH)
                    for p in range(PH):
                        row, shift = (p + PAD) % PH, (p + PAD) // PH
                        sp.dma_start(win[row * GC:(row + 1) * GC, c, :, shift:shift + NJ],
                                     phases[p]).then_inc(win_in[c], 16)

                def load_x1(t, r, c):
                    sp.wait_ge(x1_stored[c], 16 * (r + 1))
                    if live(t - 2):
                        sp.wait_ge(result_ready, 2 * (t - 1))
                    sp.dma_start(x1_res[:, c, :, :].rearrange("p q j -> p (q j)"), x1_d[t]).then_inc(x1_in[c], 16)

                def store_result(t, r, c):
                    sp.wait_ge(result_ready, 2 * (t + 1))
                    sp.dma_start(out_rows[t], result[:, c, :]).then_inc(out_stored[c], 16)

                def step(r, c):
                    if live(at(r, c, 2)[0]):
                        store_x1(*at(r, c, 2))
                    if live(at(r, c, 4)[0]):
                        load_attention(*at(r, c, 4))
                    if live(at(r, c, 2)[0]):
                        load_window(*at(r, c, 2))
                    if live(at(r, c, 1)[0]):
                        load_x1(*at(r, c, 1))
                    if live(at(r, c, 0)[0]):
                        store_result(*at(r, c, 0))

                sp.wait_ge(edges, 4)
                load_attention(0, 0, 0)
                run_steps(sp, step, FIRST, LOOP, ENDS, LAST)
                for c in range(2):
                    sp.wait_ge(out_stored[c], 16 * (PAIRS // 2))

            @block.gpsimd
            def _(pool):
                for c in range(2):
                    nc.gpsimd.memset(win[0:P // 2, c, :, 0:1], 0.0).then_inc(edges, 1)
                    pool.wait_ge(edges, 2 * c + 1)
                    nc.gpsimd.memset(win[P // 2:P, c, :, NJ:NJ + 1], 0.0).then_inc(edges, 1)
                    pool.wait_ge(edges, 2 * c + 2)

                def conv_low_part(t, r, c):
                    for b in range(2):
                        part = slice(4 * b, 4 * b + 4)
                        pool.wait_ge(conv_high, 2 * t + b + 1)
                        nc.gpsimd.tensor_tensor(conv_lo[:, c, :, part], conv[:, :, part],
                                                conv_hi[:, c, :, part].bitcast(F32), ALU.subtract).then_inc(conv_low, 1)

                def window_low_part(t, r, c):
                    pool.wait_ge(win_high, t + 1)
                    nc.gpsimd.tensor_tensor(win_lo[:, c], win[:, c], win_hi[:, c].bitcast(F32),
                                            ALU.subtract).then_inc(win_low, 1)

                def step(r, c):
                    if live(at(r, c, 1)[0]):
                        conv_low_part(*at(r, c, 1))
                    if live(at(r, c, 2)[0]):
                        window_low_part(*at(r, c, 2))

                run_steps(pool, step, FIRST, LOOP, ENDS, LAST)

            @block.scalar
            def _(act):
                def conv_high_part(t, r, c):
                    if live(t - 2):
                        act.wait_ge(ffn_acc, 2 * (t - 1))
                    for b in range(2):
                        part = slice(4 * b, 4 * b + 4)
                        act.wait_ge(conv_added, 2 * t + b + 1)
                        nc.scalar.activation(conv_hi[:, c, :, part], conv[:, :, part], ACT.Copy).then_inc(conv_high, 1)

                def values_high_part(t, r, c):
                    act.wait_ge(attn_in[c], 32 * (r + 1))
                    if live(t - 2):
                        act.wait_ge(out_acc, 2 * (t - 1))
                    nc.scalar.activation(vals_hi[:, c], vals[:, c], ACT.Copy).then_inc(vals_high, 1)

                def window_high_part(t, r, c):
                    act.wait_ge(win_in[c], 16 * PH * (r + 1))
                    if live(t - 2):
                        act.wait_ge(conv_acc, 2 * (t - 1))
                    nc.scalar.activation(win_hi[:, c], win[:, c], ACT.Copy).then_inc(win_high, 1)

                def step(r, c):
                    if live(at(r, c, 1)[0]):
                        conv_high_part(*at(r, c, 1))
                    if live(at(r, c, 3)[0]):
                        values_high_part(*at(r, c, 3))
                    if live(at(r, c, 2)[0]):
                        window_high_part(*at(r, c, 2))

                run_steps(act, step, FIRST, LOOP, ENDS, LAST)

            @block.vector
            def _(dve):
                def values_low_part(t, r, c):
                    dve.wait_ge(vals_high, t + 1)
                    nc.vector.tensor_tensor(vals_lo[:, c], vals[:, c], vals_hi[:, c].bitcast(F32),
                                            ALU.subtract).then_inc(vals_low, 1)
                    nc.vector.tensor_tensor(x_sb[:, c, :], x_sb[:, c, :], bo_sb[:, :], ALU.add).then_inc(x_biased, 1)

                def add_x(t, r, c):
                    dve.wait_ge(x_biased, t + 1)
                    if live(t - 2):
                        dve.wait_ge(x1_stored[c], 16 * r)
                    x_phases = x_sb[:, c, :].rearrange("p (j q) -> p q j", q=PH)
                    for b in range(2):
                        part = slice(H4 * b, H4 * b + H4)
                        dve.wait_ge(out_acc, 2 * t + b + 1)
                        nc.vector.tensor_tensor(x1[:, c, part, :], out_ps[b][:, :].rearrange("p (q j) -> p q j", j=NJ),
                                                x_phases[:, part, :], ALU.add).then_inc(x1_ready, 1)

                def add_conv_bias(t, r, c):
                    dve.wait_ge(convb_in[c], 16 * (r + 1))
                    for b in range(2):
                        part = slice(4 * b, 4 * b + 4)
                        dve.wait_ge(conv_acc, 2 * t + b + 1)
                        if live(t - 1):
                            dve.wait_ge(conv_low, 2 * t + b - 1)
                        nc.vector.tensor_tensor(conv[:, :, part].rearrange("p q g o -> p g q o"),
                                                conv_ps[b][:, :].rearrange("p (g q o) -> p g q o", g=4, q=PH),
                                                convb_sb[:, c, part, :].unsqueeze(2).to_broadcast([P, 4, PH, GC]),
                                                ALU.add).then_inc(conv_added, 1)

                def finish(t, r, c):
                    dve.wait_ge(x1_in[c], 16 * (r + 1))
                    if live(t - 2):
                        dve.wait_ge(out_stored[c], 16 * r)
                    for b in range(2):
                        cols = slice(b * BANK, (b + 1) * BANK)
                        dve.wait_ge(ffn_acc, 2 * t + b + 1)
                        nc.vector.scalar_tensor_tensor(
                            out=result[:, c, cols].rearrange("p (j q) -> p j q", q=PH),
                            in0=ffn_ps[b][:, :].rearrange("p (j q) -> p j q", q=PH), scalar=scale_sb[:, 0:1],
                            in1=x1_res[:, c, :, b * (NJ // 2):(b + 1) * (NJ // 2)].rearrange("p q j -> p j q"),
                            op0=ALU.mult, op1=ALU.add).then_inc(result_ready, 1)

                def step(r, c):
                    if live(at(r, c, 2)[0]):
                        add_x(*at(r, c, 2))
                    if live(at(r, c, 1)[0]):
                        add_conv_bias(*at(r, c, 1))
                    if live(at(r, c, 3)[0]):
                        values_low_part(*at(r, c, 3))
                    if live(at(r, c, 0)[0]):
                        finish(*at(r, c, 0))

                run_steps(dve, step, FIRST, LOOP, ENDS, LAST)

            @block.tensor
            def _(pe):
                def project(t, r, c):
                    pe.wait_ge(vals_low, t + 1)
                    for b in range(2):
                        if live(t - 1):
                            pe.wait_ge(x1_ready, 2 * t + b - 1)
                        n = 0
                        for a in range(HP):
                            for v, w in ((vals_hi, wo_hi), (vals_hi, wo_lo), (vals_lo, wo_hi)):
                                last = pe.matmul(out_ps[b][:, :], v[:, c, a, :], w[:, a, b * BANK:(b + 1) * BANK],
                                                 start=(n == 0), stop=(n == 3 * HP - 1))
                                n += 1
                        last.then_inc(out_acc, 1)

                def convolve(t, r, c):
                    pe.wait_ge(win_low, t + 1)
                    for g in range(BG):
                        if g % 4 == 0 and live(t - 1):
                            pe.wait_ge(conv_added, 2 * t + g // 4 - 1)
                        n = 0
                        for d in range(2):
                            for w, m in ((win_hi, band_hi), (win_hi, band_lo), (win_lo, band_hi)):
                                last = pe.matmul(conv_ps[g // 4][:, (g % 4) * P:(g % 4 + 1) * P],
                                                 w[:, c, g, d:d + NJ], m[:, d, g % GROUPS, :],
                                                 start=(n == 0), stop=(n == 5))
                                n += 1
                        if g % 4 == 3:
                            last.then_inc(conv_acc, 1)

                def feed(t, r, c):
                    pe.wait_ge(conv_low, 2 * (t + 1))
                    for b in range(2):
                        if live(t - 1):
                            pe.wait_ge(result_ready, 2 * t + b - 1)
                        n = 0
                        for p in range(PH):
                            for m in (conv_hi, conv_lo):
                                last = pe.matmul(ffn_ps[b][:, :], m[:, c, p].rearrange("p g o -> p (g o)"), signs[:, p, b * BANK:(b + 1) * BANK],
                                                 start=(n == 0), stop=(n == 2 * PH - 1))
                                n += 1
                        last.then_inc(ffn_acc, 1)

                def step(r, c):
                    if live(at(r, c, 2)[0]):
                        project(*at(r, c, 2))
                    if live(at(r, c, 1)[0]):
                        convolve(*at(r, c, 1))
                    if live(at(r, c, 0)[0]):
                        feed(*at(r, c, 0))

                run_steps(pe, step, FIRST, LOOP, ENDS, LAST)


_INS = ['x', 'cond_128', 'fside_S_0', 'L0_cond_W0', 'L0_cond_b0', 'L0_cond_W1', 'L0_cond_b1', 'L0_cond_W2',
        'L0_cond_b2', 'L0_cond_weight', 'L0_cond_bias_k', 'L0_attn_w_qkv', 'L0_attn_b_qkv', 'L0_attn_w_o',
        'L0_attn_b_o', 'L0_cond2_weight', 'L0_cond2_c_weight', 'L0_ffn_kernel', 'L0_ffn_scale']


def kernel(**inputs):
    import numpy as _np
    import concourse.bacc as _bacc
    from concourse import mybir as _mybir
    from concourse.bass_utils import run_bass_kernel_spmd as _run

    nc = _bacc.Bacc("TRN2", target_bir_lowering=False, num_devices=1)
    arrays, args = {}, []
    for name in _INS:
        a = _np.ascontiguousarray(inputs[name])
        if name == 'L0_ffn_scale':
            a = a.reshape(1, 1)
        arrays[f"in_{name}_dram"] = a
        args.append(nc.dram_tensor(f"in_{name}_dram", a.shape, _mybir.dt.from_np(a.dtype), kind="ExternalInput").ap())
    args.append(nc.dram_tensor("out_0_dram", (BATCH, SEQ, HID), F32, kind="ExternalOutput").ap())
    build(nc, *args)
    r = _run(nc, [arrays], core_ids=[0])
    return r.results[0]["out_0_dram"]
```

```python
from contextlib import ExitStack

import numpy as np

import concourse.bass as bass
from concourse import mybir

F32 = mybir.dt.float32
F32R = mybir.dt.float32r
U8 = mybir.dt.uint8
ALU = mybir.AluOpType
ACT = mybir.ActivationFunctionType
AX = mybir.AxisListType

P = 128
BATCH, SEQ, HID = 128, 64, 1024
PAIRS = BATCH // 2
HC = HID // P
HEADS, HEAD = 8, 64
PART = HEADS * HEAD
HP = HEADS // 2
QKV = 3 * PART
EXPERTS = 8
TAPS, PAD = 9, 4
GROUPS = 4
GC = SEQ // GROUPS
PH = P // GC
NJ = HID // PH
BG = 2 * GROUPS
BANK = 512
MASKED = -10000.0


def live(t):
    return not isinstance(t, int) or 0 <= t < PAIRS


def at(r, c, d):
    r2, c2 = r + (c + d) // 2, (c + d) % 2
    return 2 * r2 + c2, r2, c2


def run_steps(eng, step, first, loop_from, loop_to, last):
    for s in range(first, loop_from):
        step(s // 2, s % 2)
    with eng.Fori(loop_from // 2, loop_to // 2) as r:
        step(r, 0)
        step(r, 1)
    for s in range(loop_to, last + 1):
        step(s // 2, s % 2)


def build(nc, x, cond, fside, w0, b0, w1, b1, w2, b2, experts, bias_k,
          w_qkv, b_qkv, w_o, b_o, conv_w, ctx_w, ffn_k, ffn_scale, out):
    x_rows = x.rearrange("(t b) i h -> t (b i) h", b=2)
    out_rows = out.rearrange("(t b) i h -> t (b i) h", b=2)

    mix_d = nc.dram_tensor("mix_d", [BATCH, SEQ, SEQ], F32, kind="Internal").ap()
    aggb_d = nc.dram_tensor("aggb_d", [PAIRS, 1, 2 * SEQ], F32, kind="Internal").ap()
    convb_d = nc.dram_tensor("convb_d", [PAIRS, 1, 2 * SEQ], F32, kind="Internal").ap()
    vals_d = nc.dram_tensor("vals_d", [PAIRS, P, HP * P], F32, kind="Internal").ap()
    x1_d = nc.dram_tensor("x1_d", [PAIRS, P, HID], F32, kind="Internal").ap()

    with ExitStack() as whole:
        def sb(name, shape, dt=F32):
            return whole.enter_context(nc.sbuf_tensor(name, shape, dt))

        ident = sb("ident", [P, P])
        with ExitStack() as setup:
            setup_tiles = setup_tensors(nc, setup)
        late = Late()
        late.wo_rows = sb("wo_rows", [P, PH, PART])
        late.kernel_u8 = sb("kernel_u8", [P, PH, HID], U8)
        late.conv_rows = sb("conv_rows", [SEQ, GC, TAPS])
        late.bo = sb("bo_sb", [P, HID])
        late.scale = sb("scale_sb", [P, 1])
        late.conv_pad = sb("conv_pad", [SEQ, CK, GC])
        late.x1_res = sb("x1_res", [P, 2, PH, NJ])
        attend(nc, x_rows, cond, fside, w0, b0, w1, b1, w2, b2, experts, bias_k, ctx_w, w_qkv, b_qkv,
               w_o, b_o, conv_w, ffn_k, ffn_scale, ident, setup_tiles, late, mix_d, aggb_d, convb_d, vals_d)
        feed_forward(nc, x_rows, ident, late, convb_d, vals_d, x1_d, out_rows)


class Late:
    pass


class Setup:
    pass


CK = 24
FT = QKV // P
WB = 3
MIXES = SEQ * SEQ // BANK


def setup_tensors(nc, stack):
    def sb(name, shape, dt=F32):
        return stack.enter_context(nc.sbuf_tensor(name, shape, dt))

    s = Setup()
    s.tri = sb("tri", [P, P])
    s.cond = sb("cond_sb", [BATCH, P])
    s.w0 = sb("w0_sb", [P, P])
    s.w1 = sb("w1_sb", [P, P])
    s.w2 = sb("w2_sb", [P, EXPERTS])
    s.b0 = sb("b0_sb", [P, 1])
    s.b1 = sb("b1_sb", [P, 1])
    s.b2 = sb("b2_sb", [BATCH, EXPERTS])
    s.bias_k = sb("bk_sb", [EXPERTS, SEQ])
    s.ctx_w = sb("ctxw_sb", [SEQ, P])
    s.fside = sb("fside_sb", [BATCH, SEQ])
    s.experts = sb("exp_w", [EXPERTS, SEQ, SEQ])
    s.w_rows = sb("w_rows", [P, WB, HID])
    s.cond_t = sb("cond_t", [P, BATCH])
    s.ctxw_t = sb("ctxw_t", [P, SEQ])
    s.h1 = sb("h1", [P, BATCH])
    s.h2 = sb("h2", [P, BATCH])
    s.logits = sb("logits", [BATCH, EXPERTS])
    s.neg_max = sb("neg_max", [BATCH, 1])
    s.att_sum = sb("att_sum", [BATCH, 1])
    s.att_inv = sb("att_inv", [BATCH, 1])
    s.att_e = sb("att_e", [BATCH, EXPERTS])
    s.att = sb("att", [BATCH, EXPERTS])
    s.att_t = sb("att_t", [EXPERTS, BATCH])
    s.aggb = sb("aggb", [BATCH, SEQ])
    s.convb = sb("convb", [BATCH, SEQ])
    s.mix = sb("mix", [BATCH, 2, BANK])
    return s


def attend(nc, x_rows, cond, fside, w0, b0, w1, b1, w2, b2, experts, bias_k, ctx_w, w_qkv, b_qkv,
           w_o, b_o, conv_w, ffn_k, ffn_scale, ident, st, late, mix_d, aggb_d, convb_d, vals_d):
    with ExitStack() as ctx:
        def sb(name, shape, dt=F32):
            return ctx.enter_context(nc.sbuf_tensor(name, shape, dt))

        def bank(name):
            return ctx.enter_context(nc.psum_tensor(name, [P, BANK], F32))

        def sem(name):
            return ctx.enter_context(nc.semaphore(name))

        w_hi = sb("w_hi", [P, HC, QKV], F32R)
        w_lo = sb("w_lo", [P, HC, QKV], F32R)
        mask = sb("mask", [P, SEQ])
        masked = sb("masked", [P, SEQ])
        bias_sb = sb("bias_sb", [P, QKV])
        x_sb = sb("x_sb", [P, 2, HID])
        mix_sb = sb("mix_sb", [P, 2, P])
        aggb_sb = sb("aggb_sb", [P, 2, P])
        y_sum = sb("y_sum", [P, HC, P])
        y_hi = sb("y_hi", [P, 2, HC, P], F32R)
        y_lo = sb("y_lo", [P, 2, HC, P], F32R)
        qk = sb("qk", [P, 2, PART])
        v_sb = sb("v_sb", [P, 2, PART])
        qk_t = sb("qk_t", [P, 2, HP, P])
        scores = sb("scores", [P, HEADS, SEQ])
        row_max = sb("row_max", [P, HEADS])
        exps = sb("exps", [P, HEADS, SEQ])
        row_sum = sb("row_sum", [P, HEADS])
        row_inv = sb("row_inv", [P, HEADS])
        probs = sb("probs", [P, HEADS, P])
        probs_t = sb("probs_t", [P, HEADS, P])
        vals = sb("vals", [P, 2, HP, P])

        qkv_ps = [bank("qkv_ps0"), bank("qkv_ps1")]
        y_ps = [bank("y_ps0"), bank("y_ps1")]
        score_ps = [bank("score_ps0"), bank("score_ps1")]
        turn_ps = [bank("turn_ps0"), bank("turn_ps1")]

        inputs_in = [sem("inputs_in0"), sem("inputs_in1")]
        bias_in, cleared = sem("bias_in"), sem("cleared")
        y_acc, y_added, y_high, y_low = sem("y_acc"), sem("y_added"), sem("y_high"), sem("y_low")
        qkv_acc, qkv_out = sem("qkv_acc"), sem("qkv_out")
        turned, qk_t_out = sem("turned"), sem("qk_t_out")
        scores_acc, scores_cut, scores_masked = sem("scores_acc"), sem("scores_cut"), sem("scores_masked")
        maxed, shifted, exped, summed, inverted = (sem("maxed"), sem("shifted"), sem("exped"), sem("summed"),
                                                   sem("inverted"))
        probs_ready, probs_turned, probs_t_out = sem("probs_ready"), sem("probs_turned"), sem("probs_t_out")
        vals_acc, vals_out = sem("vals_acc"), sem("vals_out")
        vals_stored = [sem("vals_stored0"), sem("vals_stored1")]

        FIRST, LOOP, ENDS, LAST = -1, 4, PAIRS - 2, PAIRS + 1

        loaded, experts_in = sem("loaded"), sem("experts_in")
        rows_in = [sem(f"rows_in{n}") for n in range(WB)]
        zeroed, consts, masks = sem("zeroed"), sem("consts"), sem("masks")
        chain_pe, chain_act, chain_dve = sem("chain_pe"), sem("chain_act"), sem("chain_dve")
        mix_acc, mix_out = sem("mix_acc"), sem("mix_out")
        mix_stored = [sem("mix_stored0"), sem("mix_stored1")]
        biases_stored, late_in = sem("biases_stored"), sem("late_in")
        wt_acc, wt_hi, wt_lo = sem("wt_acc"), sem("wt_hi"), sem("wt_lo")
        wt_ps = [score_ps[0], score_ps[1], turn_ps[0], turn_ps[1]]
        mix_ps = [y_ps[0], y_ps[1]]

        def wt_out(w, n):
            f, half = n // 2, n % 2
            return w[:, 4 * half:4 * half + 4, f * P:(f + 1) * P]

        with nc.Block() as block:
            @block.sync
            def _(sp):
                for f in range(FT):
                    if f >= WB:
                        sp.wait_ge(wt_acc, 2 * (f - WB + 1))
                    sp.dma_start(st.w_rows[:, f % WB, :], w_qkv[f * P:(f + 1) * P, :]).then_inc(rows_in[f % WB], 16)
                    if f == WB - 1:
                        sp.dma_start(st.experts[:, :, :], experts.rearrange("k o i a -> k o (i a)")).then_inc(experts_in, 16)
                sp.dma_start(bias_sb[:, :], b_qkv.rearrange("(a n) -> a n", a=1).to_broadcast([P, QKV])).then_inc(bias_in, 16)
                for c in range(2):
                    sp.wait_ge(mix_stored[c], 16 * MIXES // 2)
                sp.wait_ge(biases_stored, 32)

                def load_late():
                    sp.wait_ge(wt_acc, 2 * FT)
                    for dst, src in ((late.wo_rows[:, :, :], w_o.rearrange("(j p) n -> j p n", p=PH)),
                                     (late.kernel_u8[:, :, :], ffn_k.rearrange("(j p) f -> j p f", p=PH)),
                                     (late.conv_rows[:, :, :], conv_w),
                                     (late.scale[:, :], ffn_scale.to_broadcast([P, 1])),
                                     (late.bo[:, :], b_o.rearrange("(a n) -> a n", a=1).to_broadcast([P, HID]))):
                        sp.dma_start(dst, src).then_inc(late_in, 16)

                def load(t, r, c):
                    if live(t - 2):
                        sp.wait_ge(y_added, 2 * (t - 1))
                    sp.dma_start(x_sb[:, c, :], x_rows[t]).then_inc(inputs_in[c], 16)
                    for b in range(2):
                        half = slice(SEQ * b, SEQ * b + SEQ)
                        sp.dma_start(mix_sb[half, c, half], mix_pairs[t, half, :]).then_inc(inputs_in[c], 16)
                    sp.dma_start(aggb_sb[:, c, :], aggb_d[t].to_broadcast([P, P])).then_inc(inputs_in[c], 16)

                def store(t, r, c):
                    sp.wait_ge(vals_out, t + 1)
                    sp.dma_start(vals_d[t], vals[:, c, :, :].rearrange("p a n -> p (a n)")).then_inc(vals_stored[c], 16)

                def step(r, c):
                    if live(at(r, c, 2)[0]):
                        load(*at(r, c, 2))
                    if live(at(r, c, -2)[0]):
                        store(*at(r, c, -2))
                    if isinstance(r, int) and at(r, c, 0)[0] == 1:
                        load_late()

                mix_pairs = mix_d.rearrange("(t b) i o -> t (b i) o", b=2)
                sp.wait_ge(cleared, 3)
                load(0, 0, 0)
                run_steps(sp, step, FIRST, LOOP, ENDS, LAST)
                sp.wait_ge(late_in, 80)
                for c in range(2):
                    sp.wait_ge(vals_stored[c], 16 * (PAIRS // 2))

            @block.gpsimd
            def _(pool):
                nc.gpsimd.memset(ident[:, :], 0.0).then_inc(zeroed, 1)
                nc.gpsimd.memset(st.tri[:, :], 1.0).then_inc(zeroed, 1)
                pool.wait_ge(zeroed, 2)
                nc.gpsimd.affine_select(out=ident[:, :], in_=ident[:, :], compare_op=ALU.not_equal, fill=1.0,
                                        base=0, pattern=[[-1, P]], channel_multiplier=1).then_inc(consts, 1)
                nc.gpsimd.affine_select(out=st.tri[:, :], in_=st.tri[:, :], compare_op=ALU.is_ge, fill=0.0,
                                        base=0, pattern=[[-1, P]], channel_multiplier=1).then_inc(consts, 1)
                nc.gpsimd.memset(mix_sb[:, 0, :], 0.0).then_inc(cleared, 1)
                nc.gpsimd.memset(mix_sb[:, 1, :], 0.0).then_inc(cleared, 1)
                nc.gpsimd.memset(probs[:, :, :], 0.0).then_inc(cleared, 1)

                def add_masked(t, r, c):
                    pool.wait_ge(scores_cut, t + 1)
                    nc.gpsimd.tensor_tensor(scores[:, :, :], scores[:, :, :],
                                            masked[:, :].unsqueeze(1).to_broadcast([P, HEADS, SEQ]),
                                            ALU.add).then_inc(scores_masked, 1)

                def low_part(t, r, c):
                    for b in range(2):
                        chunks = slice(4 * b, 4 * b + 4)
                        pool.wait_ge(y_high, 2 * t + b + 1)
                        nc.gpsimd.tensor_tensor(y_lo[:, c, chunks, :], y_sum[:, chunks, :],
                                                y_hi[:, c, chunks, :].bitcast(F32), ALU.subtract).then_inc(y_low, 1)

                def step(r, c):
                    if live(at(r, c, -1)[0]):
                        add_masked(*at(r, c, -1))
                    if live(at(r, c, 1)[0]):
                        low_part(*at(r, c, 1))

                run_steps(pool, step, FIRST, LOOP, ENDS, LAST)

            @block.scalar
            def _(act):
                for dst, src in ((st.cond[:, :], cond), (st.ctx_w[:, :], ctx_w), (st.w0[:, :], w0),
                                 (st.b0[:, :], b0.rearrange("(p a) -> p a", a=1)), (st.w1[:, :], w1),
                                 (st.b1[:, :], b1.rearrange("(p a) -> p a", a=1)), (st.w2[:, :], w2),
                                 (st.b2[:, :], b2.rearrange("(a k) -> a k", a=1).to_broadcast([BATCH, EXPERTS])),
                                 (st.bias_k[:, :], bias_k),
                                 (st.fside[:, :], fside.rearrange("(a k) -> a k", a=1).to_broadcast([BATCH, SEQ]))):
                    act.dma_start(dst, src).then_inc(loaded, 16)

                def gate(k):
                    if k == 1:
                        act.wait_ge(chain_pe, 2)
                        nc.scalar.activation(st.h1[:, :], qkv_ps[1][:, 0:BATCH], ACT.Gelu,
                                             bias=st.b0[:, 0:1]).then_inc(chain_act, 1)
                    if k == 2:
                        act.wait_ge(chain_pe, 3)
                        nc.scalar.activation(st.h2[:, :], qkv_ps[0][:, 0:BATCH], ACT.Gelu,
                                             bias=st.b1[:, 0:1]).then_inc(chain_act, 1)
                    if k == 3:
                        act.wait_ge(chain_dve, 4)
                        nc.scalar.activation(st.att_e[:, :], st.logits[:, :], ACT.Exp, bias=st.neg_max[:, 0:1],
                                             accum_out=st.att_sum[:, 0:1]).then_inc(chain_act, 1)
                    if k == 5:
                        act.wait_ge(chain_dve, 9)
                        act.dma_start(aggb_d.rearrange("t a (b o) -> (t a b) o", b=2), st.aggb[:, :]).then_inc(biases_stored, 16)
                        act.dma_start(convb_d.rearrange("t a (b o) -> (t a b) o", b=2), st.convb[:, :]).then_inc(biases_stored, 16)
                    if k in (6, 7):
                        for n in range(4 * (k - 6), 4 * (k - 6) + 4):
                            act.wait_ge(mix_acc, n + 1)
                            if n >= 2:
                                act.wait_ge(mix_stored[n % 2], 16 * (n // 2))
                            nc.scalar.activation(st.mix[:, n % 2, :], mix_ps[n % 2][:, :], ACT.Copy).then_inc(mix_out, 1)
                            act.wait_ge(mix_out, n + 1)
                            act.dma_start(mix_d.rearrange("b i o -> b (i o)")[:, n * BANK:(n + 1) * BANK],
                                          st.mix[:, n % 2, :]).then_inc(mix_stored[n % 2], 16)

                for f in range(FT):
                    for n in (2 * f, 2 * f + 1):
                        act.wait_ge(wt_acc, n + 1)
                        nc.scalar.activation(wt_out(w_hi, n), wt_ps[n % 4][:, :].rearrange("p (q f) -> p q f", q=4),
                                             ACT.Copy).then_inc(wt_hi, 1)
                    gate(f)

                def values_out(t, r, c):
                    act.wait_ge(vals_acc, t + 1)
                    if live(t - 2):
                        act.wait_ge(vals_stored[c], 16 * r)
                    nc.scalar.activation(vals[:, c, :, :], turn_ps[0][:, :].rearrange("p (a n) -> p a n", a=HP),
                                         ACT.Copy).then_inc(vals_out, 1)

                def exponent(t, r, c):
                    act.wait_ge(shifted, t + 1)
                    if live(t - 1):
                        act.wait_ge(probs_ready, t)
                    nc.scalar.activation(exps[:, :, :], scores[:, :, :], ACT.Exp).then_inc(exped, 1)

                def high_part(t, r, c):
                    if live(t - 2):
                        act.wait_ge(qkv_acc, 3 * (t - 1))
                    for b in range(2):
                        chunks = slice(4 * b, 4 * b + 4)
                        act.wait_ge(y_added, 2 * t + b + 1)
                        nc.scalar.activation(y_hi[:, c, chunks, :], y_sum[:, chunks, :], ACT.Copy).then_inc(y_high, 1)

                def qk_turned_out(t, r, c):
                    if live(t - 1):
                        act.wait_ge(scores_acc, t)
                    for j in range(2):
                        act.wait_ge(turned, 2 * t + j + 1)
                        nc.scalar.activation(qk_t[:, j, :, :], turn_ps[j][:, :].rearrange("p (a n) -> p a n", a=HP),
                                             ACT.Copy).then_inc(qk_t_out, 1)

                def probs_turned_out(t, r, c):
                    if live(t - 1):
                        act.wait_ge(vals_acc, t)
                    for b in range(2):
                        act.wait_ge(probs_turned, 2 * t + b + 1)
                        nc.scalar.activation(probs_t[:, 4 * b:4 * b + 4, :],
                                             y_ps[b][:, :].rearrange("p (a n) -> p a n", a=4),
                                             ACT.Copy).then_inc(probs_t_out, 1)

                def step(r, c):
                    if live(at(r, c, -2)[0]):
                        values_out(*at(r, c, -2))
                    if live(at(r, c, -1)[0]):
                        exponent(*at(r, c, -1))
                    if live(at(r, c, 1)[0]):
                        high_part(*at(r, c, 1))
                    if live(at(r, c, 0)[0]):
                        qk_turned_out(*at(r, c, 0))
                    if live(at(r, c, -1)[0]):
                        probs_turned_out(*at(r, c, -1))

                run_steps(act, step, FIRST, LOOP, ENDS, LAST)

            @block.vector
            def _(dve):
                dve.wait_ge(consts, 2)
                for b in range(2):
                    rows = slice(SEQ * b, SEQ * b + SEQ)
                    last = nc.vector.tensor_copy(mask[rows, :], st.tri[rows, rows])
                last.then_inc(masks, 1)
                dve.wait_ge(masks, 1)
                nc.vector.tensor_scalar(masked[:, :], mask[:, :], -MASKED, MASKED, ALU.mult, ALU.add).then_inc(masks, 1)

                def gate(k):
                    if k == 0:
                        dve.wait_ge(chain_pe, 1)
                        nc.vector.tensor_copy(st.cond_t[:, :], qkv_ps[0][:, 0:BATCH]).then_inc(chain_dve, 1)
                        nc.vector.tensor_copy(st.ctxw_t[:, :], qkv_ps[0][:, P:P + SEQ]).then_inc(chain_dve, 1)
                    if k == 3:
                        dve.wait_ge(chain_pe, 4)
                        nc.vector.tensor_tensor(st.logits[:, :], qkv_ps[1][:, 0:EXPERTS], st.b2[:, :],
                                                ALU.add).then_inc(chain_dve, 1)
                        dve.wait_ge(chain_dve, 3)
                        nc.vector.tensor_reduce(st.neg_max[:, :], st.logits[:, :], AX.X, ALU.max,
                                                negate=True).then_inc(chain_dve, 1)
                        dve.wait_ge(chain_act, 3)
                        nc.vector.reciprocal(st.att_inv[:, :], st.att_sum[:, :]).then_inc(chain_dve, 1)
                        dve.wait_ge(chain_dve, 5)
                        nc.vector.tensor_scalar(st.att[:, :], st.att_e[:, :], st.att_inv[:, 0:1], None,
                                                ALU.mult).then_inc(chain_dve, 1)
                    if k == 4:
                        dve.wait_ge(chain_pe, 5)
                        nc.vector.tensor_copy(st.att_t[:, :], qkv_ps[0][0:EXPERTS, 0:BATCH]).then_inc(chain_dve, 1)
                    if k == 5:
                        dve.wait_ge(chain_pe, 7)
                        nc.vector.tensor_copy(st.aggb[:, :], qkv_ps[1][:, 0:SEQ]).then_inc(chain_dve, 1)
                        nc.vector.tensor_tensor(st.convb[:, :], qkv_ps[0][:, 0:SEQ], st.fside[:, :],
                                                ALU.add).then_inc(chain_dve, 1)

                for f in range(FT):
                    for n in (2 * f, 2 * f + 1):
                        dve.wait_ge(wt_hi, n + 1)
                        nc.vector.tensor_tensor(wt_out(w_lo, n), wt_ps[n % 4][:, :].rearrange("p (q f) -> p q f", q=4),
                                                wt_out(w_hi, n).bitcast(F32), ALU.subtract).then_inc(wt_lo, 1)
                    gate(f)
                dve.wait_ge(bias_in, 16)
                dve.wait_ge(cleared, 3)

                def qkv_part_out(t, r, c, j):
                    dve.wait_ge(qkv_acc, 3 * t + j + 1)
                    if j < 2:
                        if live(t - 1):
                            dve.wait_ge(turned, 2 * t + j - 1)
                        dst = qk[:, j, :]
                    else:
                        if live(t - 2):
                            dve.wait_ge(vals_acc, t - 1)
                        dst = v_sb[:, c, :]
                    nc.vector.tensor_tensor(dst, qkv_ps[(c + j) % 2][:, :], bias_sb[:, j * PART:(j + 1) * PART],
                                            ALU.add).then_inc(qkv_out, 1)

                def softmax(t, r, c):
                    dve.wait_ge(scores_acc, t + 1)
                    if live(t - 1):
                        dve.wait_ge(exped, t)
                    for parity in range(2):
                        last = nc.vector.tensor_tensor(
                            scores[:, HP * parity:HP * parity + HP, :],
                            score_ps[parity][:, 0:HP * SEQ].rearrange("p (a f) -> p a f", a=HP),
                            mask[:, :].unsqueeze(1).to_broadcast([P, HP, SEQ]), ALU.mult)
                    last.then_inc(scores_cut, 1)
                    dve.wait_ge(scores_masked, t + 1)
                    nc.vector.tensor_reduce(row_max[:, :], scores[:, :, :], AX.X, ALU.max).then_inc(maxed, 1)
                    dve.wait_ge(maxed, t + 1)
                    nc.vector.tensor_tensor(scores[:, :, :], scores[:, :, :],
                                            row_max[:, :].unsqueeze(2).to_broadcast([P, HEADS, SEQ]),
                                            ALU.subtract).then_inc(shifted, 1)
                    dve.wait_ge(exped, t + 1)
                    nc.vector.tensor_reduce(row_sum[:, :], exps[:, :, :], AX.X, ALU.add).then_inc(summed, 1)
                    dve.wait_ge(summed, t + 1)
                    nc.vector.reciprocal(row_inv[:, :], row_sum[:, :]).then_inc(inverted, 1)

                def normalise(t, r, c):
                    dve.wait_ge(inverted, t + 1)
                    if live(t - 1):
                        dve.wait_ge(probs_turned, 2 * t)
                    for b in range(2):
                        half = slice(SEQ * b, SEQ * b + SEQ)
                        for parity in range(2):
                            heads = slice(HP * parity, HP * parity + HP)
                            last = nc.vector.tensor_tensor(
                                probs[half, :, half].rearrange("p (a e) f -> p e a f", e=2)[:, parity],
                                exps[half, heads, :],
                                row_inv[half, heads].unsqueeze(2).to_broadcast([SEQ, HP, SEQ]), ALU.mult)
                    last.then_inc(probs_ready, 1)

                def add_bias(t, r, c):
                    for b in range(2):
                        chunks = slice(4 * b, 4 * b + 4)
                        dve.wait_ge(y_acc, 2 * t + b + 1)
                        if live(t - 1):
                            dve.wait_ge(y_low, 2 * t + b - 1)
                        nc.vector.tensor_tensor(y_sum[:, chunks, :], y_ps[b][:, :].rearrange("p (a n) -> p a n", a=4),
                                                aggb_sb[:, c, :].unsqueeze(1).to_broadcast([P, 4, P]),
                                                ALU.add).then_inc(y_added, 1)

                def step(r, c):
                    t = at(r, c, 0)[0]
                    if live(t):
                        qkv_part_out(*at(r, c, 0), 0)
                    if live(at(r, c, -1)[0]):
                        softmax(*at(r, c, -1))
                        normalise(*at(r, c, -1))
                    if live(t):
                        qkv_part_out(*at(r, c, 0), 1)
                    if live(at(r, c, 1)[0]):
                        add_bias(*at(r, c, 1))
                    if live(t):
                        qkv_part_out(*at(r, c, 0), 2)

                run_steps(dve, step, FIRST, LOOP, ENDS, LAST)

            @block.tensor
            def _(pe):
                def gate(k):
                    if k == 0:
                        pe.wait_ge(loaded, 160)
                        pe.transpose(qkv_ps[0][:, 0:BATCH], st.cond[:, :], ident[:, :])
                        pe.transpose(qkv_ps[0][:, P:P + SEQ], st.ctx_w[:, :], ident[0:SEQ, 0:SEQ]).then_inc(chain_pe, 1)
                    if k == 1:
                        pe.wait_ge(chain_dve, 2)
                        pe.matmul(qkv_ps[1][:, 0:BATCH], st.w0[:, :], st.cond_t[:, :], start=True, stop=True).then_inc(chain_pe, 1)
                    if k == 2:
                        pe.wait_ge(chain_act, 1)
                        pe.matmul(qkv_ps[0][:, 0:BATCH], st.w1[:, :], st.h1[:, :], start=True, stop=True).then_inc(chain_pe, 1)
                    if k == 3:
                        pe.wait_ge(chain_act, 2)
                        pe.matmul(qkv_ps[1][:, 0:EXPERTS], st.h2[:, :], st.w2[:, :], start=True, stop=True).then_inc(chain_pe, 1)
                    if k == 4:
                        pe.wait_ge(chain_dve, 6)
                        pe.transpose(qkv_ps[0][0:EXPERTS, 0:BATCH], st.att[:, :], ident[:, :]).then_inc(chain_pe, 1)
                    if k == 5:
                        pe.wait_ge(chain_dve, 7)
                        pe.matmul(qkv_ps[1][:, 0:SEQ], st.att_t[:, :], st.bias_k[:, :], start=True, stop=True).then_inc(chain_pe, 1)
                        pe.matmul(qkv_ps[0][:, 0:SEQ], st.cond_t[:, :], st.ctxw_t[:, :], start=True, stop=True).then_inc(chain_pe, 1)
                    if k in (6, 7):
                        pe.wait_ge(experts_in, 16)
                        ins = BANK // SEQ
                        for n in range(4 * (k - 6), 4 * (k - 6) + 4):
                            if n >= 2:
                                pe.wait_ge(mix_out, n - 1)
                            pe.matmul(mix_ps[n % 2][:, :], st.att_t[:, :],
                                      st.experts[:, :, n * ins:(n + 1) * ins].rearrange("k o i -> k i o"),
                                      start=True, stop=True).then_inc(mix_acc, 1)

                pe.wait_ge(consts, 1)
                for f in range(FT):
                    pe.wait_ge(rows_in[f % WB], 16 * (f // WB + 1))
                    for n in (2 * f, 2 * f + 1):
                        if n >= 4:
                            pe.wait_ge(wt_lo, n - 3)
                        for q in range(4):
                            h = 4 * (n % 2) + q
                            last = pe.transpose(wt_ps[n % 4][:, q * P:(q + 1) * P],
                                                st.w_rows[:, f % WB, h * P:(h + 1) * P], ident[:, :])
                        last.then_inc(wt_acc, 1)
                    gate(f)
                pe.wait_ge(mix_out, MIXES)
                pe.wait_ge(wt_lo, 2 * FT)

                def mix_x(t, r, c):
                    pe.wait_ge(inputs_in[c], 64 * (r + 1))
                    if live(t - 3):
                        pe.wait_ge(probs_t_out, 2 * (t - 2))
                    for h in range(HC):
                        last = pe.matmul(y_ps[h // 4][:, (h % 4) * P:(h % 4 + 1) * P], x_sb[:, c, h * P:(h + 1) * P],
                                         mix_sb[:, c, :], start=True, stop=True)
                        if h % 4 == 3:
                            last.then_inc(y_acc, 1)

                def qkv_part(t, r, c, j):
                    if j == 0:
                        pe.wait_ge(y_low, 2 * (t + 1))
                    if not isinstance(t, int) or 3 * t + j >= 2:
                        pe.wait_ge(qkv_out, 3 * t + j - 1)
                    n = 0
                    for h in range(HC):
                        for y, w in ((y_hi, w_hi), (y_hi, w_lo), (y_lo, w_hi)):
                            last = pe.matmul(qkv_ps[(c + j) % 2][:, :], y[:, c, h, :], w[:, h, j * PART:(j + 1) * PART],
                                             start=(n == 0), stop=(n == 3 * HC - 1))
                            n += 1
                    last.then_inc(qkv_acc, 1)

                def turn_qk(t, r, c):
                    if live(t - 2):
                        pe.wait_ge(vals_out, t - 1)
                    for j in range(2):
                        pe.wait_ge(qkv_out, 3 * t + j + 1)
                        for a in range(HP):
                            last = pe.transpose(turn_ps[j][:, a * P:(a + 1) * P], qk[:, j, a * P:(a + 1) * P], ident[:, :])
                        last.then_inc(turned, 1)

                def score(t, r, c):
                    pe.wait_ge(qk_t_out, 2 * (t + 1))
                    if live(t - 1):
                        pe.wait_ge(scores_cut, t)
                    pe.nop(nofuse=True)
                    for a in range(HP):
                        for b in range(2):
                            rows = slice(SEQ * b, SEQ * b + SEQ)
                            for parity in range(2):
                                head = slice(HEAD * parity, HEAD * parity + HEAD)
                                last = pe.matmul(score_ps[parity][rows, a * SEQ:(a + 1) * SEQ],
                                                 qk_t[head, 0, a, rows], qk_t[head, 1, a, rows], start=True, stop=True)
                    last.then_inc(scores_acc, 1)

                def turn_probs(t, r, c):
                    pe.wait_ge(probs_ready, t + 1)
                    pe.wait_ge(y_added, min(2 * (t + 3), 2 * PAIRS) if isinstance(t, int) else 2 * (t + 3))
                    for head in range(HEADS):
                        last = pe.transpose(y_ps[head // 4][:, (head % 4) * P:(head % 4 + 1) * P], probs[:, head, :], ident[:, :])
                        if head % 4 == 3:
                            last.then_inc(probs_turned, 1)

                def values(t, r, c):
                    pe.wait_ge(probs_t_out, 2 * (t + 1))
                    if live(t + 1):
                        pe.wait_ge(qk_t_out, 2 * t + 3)
                    pe.nop(nofuse=True)
                    for a in range(HP):
                        for parity in range(2):
                            head = 2 * a + parity
                            last = pe.matmul(turn_ps[0][HEAD * parity:HEAD * parity + HEAD, a * P:(a + 1) * P],
                                             v_sb[:, c, head * HEAD:(head + 1) * HEAD], probs_t[:, head, :],
                                             start=True, stop=True)
                    last.then_inc(vals_acc, 1)

                def step(r, c):
                    t = at(r, c, 0)[0]
                    if live(t):
                        qkv_part(*at(r, c, 0), 0)
                    if live(at(r, c, -2)[0]):
                        values(*at(r, c, -2))
                    if live(at(r, c, -1)[0]):
                        score(*at(r, c, -1))
                    if live(t):
                        qkv_part(*at(r, c, 0), 1)
                    if live(at(r, c, 1)[0]):
                        mix_x(*at(r, c, 1))
                    if live(t):
                        qkv_part(*at(r, c, 0), 2)
                        turn_qk(*at(r, c, 0))
                    if live(at(r, c, -1)[0]):
                        turn_probs(*at(r, c, -1))

                run_steps(pe, step, FIRST, LOOP, ENDS, LAST)


def feed_forward(nc, x_rows, ident, late, convb_d, vals_d, x1_d, out_rows):
    with ExitStack() as ctx:
        def sb(name, shape, dt=F32):
            return ctx.enter_context(nc.sbuf_tensor(name, shape, dt))

        def bank(name):
            return ctx.enter_context(nc.psum_tensor(name, [P, BANK], F32))

        def sem(name):
            return ctx.enter_context(nc.semaphore(name))

        wo_hi = sb("wo_hi", [P, HP, HID], F32R)
        wo_lo = sb("wo_lo", [P, HP, HID], F32R)
        signs = sb("signs", [P, PH, HID], F32R)
        bands = sb("bands", [P, 2, GROUPS, P])

        out_ps = [bank("out_ps0"), bank("out_ps1")]
        ffn_ps = [bank("ffn_ps0"), bank("ffn_ps1")]
        conv_ps = [bank("conv_ps0"), bank("conv_ps1")]
        spare_ps = [bank("spare_ps0"), bank("spare_ps1")]

        wo_turned, wo_high, wo_low = sem("wo_turned"), sem("wo_high"), sem("wo_low")
        pad_zero, padded = sem("pad_zero"), sem("padded")
        bands_turned, bands_out, signed = sem("bands_turned"), sem("bands_out"), sem("signed")
        wo_ps = ffn_ps + conv_ps

        vals = sb("vals_in", [P, 2, HP, P])
        vals_hi = sb("vals_hi", [P, 2, HP, P], F32R)
        vals_lo = sb("vals_lo", [P, 2, HP, P], F32R)
        x_sb = sb("x_res", [P, 2, HID])
        x1 = sb("x1", [P, 2, PH, NJ])
        x1_res = late.x1_res
        win = sb("win", [P, 2, BG, NJ + 1])
        convb_sb = sb("convb_sb", [P, 2, BG, GC])
        conv = sb("conv", [P, PH, BG, GC])
        conv_hi = sb("conv_hi", [P, 2, PH, BG, GC], F32R)
        conv_lo = sb("conv_lo", [P, 2, PH, BG, GC], F32R)
        result = sb("result", [P, 2, HID])

        attn_in = [sem("attn_in0"), sem("attn_in1")]
        convb_in = [sem("convb_in0"), sem("convb_in1")]
        x1_stored = [sem("x1_stored0"), sem("x1_stored1")]
        win_in = [sem("win_in0"), sem("win_in1")]
        x1_in = [sem("x1_in0"), sem("x1_in1")]
        out_stored = [sem("out_stored0"), sem("out_stored1")]
        edges = sem("edges")
        vals_high, vals_low = sem("vals_high"), sem("vals_low")
        x_biased = sem("x_biased")
        out_acc, x1_ready = sem("out_acc"), sem("x1_ready")
        conv_acc, conv_added, conv_high, conv_low = sem("conv_acc"), sem("conv_added"), sem("conv_high"), sem("conv_low")
        ffn_acc, result_ready = sem("ffn_acc"), sem("result_ready")

        FIRST, LOOP, ENDS, LAST = -3, 2, PAIRS - 4, PAIRS - 1
        H4 = PH // 2

        with nc.Block() as block:
            @block.sync
            def _(sp):
                def load_attention(t, r, c):
                    if live(t - 2):
                        sp.wait_ge(x1_ready, 2 * (t - 1))
                    sp.dma_start(vals[:, c, :, :].rearrange("p a n -> p (a n)"), vals_d[t]).then_inc(attn_in[c], 16)
                    sp.dma_start(x_sb[:, c, :], x_rows[t]).then_inc(attn_in[c], 16)

                def store_x1(t, r, c):
                    sp.wait_ge(x1_ready, 2 * (t + 1))
                    sp.dma_start(x1_d[t], x1[:, c, :, :].rearrange("p q j -> p (q j)")).then_inc(x1_stored[c], 16)

                def load_window(t, r, c):
                    if live(t - 2):
                        sp.wait_ge(conv_added, 2 * (t - 1))
                    sp.dma_start(convb_sb[:, c, :, :].rearrange("p g o -> p (g o)"),
                                 convb_d[t].to_broadcast([P, P])).then_inc(convb_in[c], 16)
                    sp.wait_ge(x1_stored[c], 16 * (r + 1))
                    phases = x1_d[t].rearrange("(g i) (p j) -> p i g j", i=GC, p=PH)
                    for p in range(PH):
                        row, shift = (p + PAD) % PH, (p + PAD) // PH
                        sp.dma_start(win[row * GC:(row + 1) * GC, c, :, shift:shift + NJ],
                                     phases[p]).then_inc(win_in[c], 16)

                def load_x1(t, r, c):
                    sp.wait_ge(x1_stored[c], 16 * (r + 1))
                    if live(t - 2):
                        sp.wait_ge(result_ready, 2 * (t - 1))
                    sp.dma_start(x1_res[:, c, :, :].rearrange("p q j -> p (q j)"), x1_d[t]).then_inc(x1_in[c], 16)

                def store_result(t, r, c):
                    sp.wait_ge(result_ready, 2 * (t + 1))
                    sp.dma_start(out_rows[t], result[:, c, :]).then_inc(out_stored[c], 16)

                def step(r, c):
                    if live(at(r, c, 2)[0]):
                        store_x1(*at(r, c, 2))
                    if live(at(r, c, 4)[0]):
                        load_attention(*at(r, c, 4))
                    if live(at(r, c, 2)[0]):
                        load_window(*at(r, c, 2))
                    if live(at(r, c, 1)[0]):
                        load_x1(*at(r, c, 1))
                    if live(at(r, c, 0)[0]):
                        store_result(*at(r, c, 0))

                sp.wait_ge(edges, 4)
                load_attention(0, 0, 0)
                run_steps(sp, step, FIRST, LOOP, ENDS, LAST)
                for c in range(2):
                    sp.wait_ge(out_stored[c], 16 * (PAIRS // 2))

            @block.gpsimd
            def _(pool):
                nc.gpsimd.memset(late.conv_pad[:, :, :], 0.0).then_inc(pad_zero, 1)
                pool.wait_ge(pad_zero, 1)
                for c in range(2):
                    nc.gpsimd.memset(win[0:P // 2, c, :, 0:1], 0.0).then_inc(edges, 1)
                    pool.wait_ge(edges, 2 * c + 1)
                    nc.gpsimd.memset(win[P // 2:P, c, :, NJ:NJ + 1], 0.0).then_inc(edges, 1)
                    pool.wait_ge(edges, 2 * c + 2)

                for p in range(PH):
                    nc.gpsimd.tensor_scalar(signs[:, p, :], late.kernel_u8[:, p, :], 2.0, -1.0,
                                            ALU.mult, ALU.add).then_inc(signed, 1)

                def conv_low_part(t, r, c):
                    for b in range(2):
                        part = slice(4 * b, 4 * b + 4)
                        pool.wait_ge(conv_high, 2 * t + b + 1)
                        nc.gpsimd.tensor_tensor(conv_lo[:, c, :, part], conv[:, :, part],
                                                conv_hi[:, c, :, part].bitcast(F32), ALU.subtract).then_inc(conv_low, 1)

                def step(r, c):
                    if live(at(r, c, 1)[0]):
                        conv_low_part(*at(r, c, 1))

                run_steps(pool, step, FIRST, LOOP, ENDS, LAST)

            @block.scalar
            def _(act):
                for p in range(PH):
                    act.wait_ge(wo_turned, p + 1)
                    nc.scalar.activation(wo_hi[:, :, p * P:(p + 1) * P],
                                         wo_ps[p % 4][:, :].rearrange("p (a n) -> p a n", a=HP),
                                         ACT.Copy).then_inc(wo_high, 1)
                for d in range(2):
                    act.wait_ge(bands_turned, d + 1)
                    nc.scalar.activation(bands[:, d, :, :].rearrange("p g (q o) -> p q g o", q=PH),
                                         spare_ps[d][:, :].rearrange("p (q g o) -> p q g o", q=PH, g=GROUPS),
                                         ACT.Copy).then_inc(bands_out, 1)

                def conv_high_part(t, r, c):
                    if live(t - 2):
                        act.wait_ge(ffn_acc, 2 * (t - 1))
                    for b in range(2):
                        part = slice(4 * b, 4 * b + 4)
                        act.wait_ge(conv_added, 2 * t + b + 1)
                        nc.scalar.activation(conv_hi[:, c, :, part], conv[:, :, part], ACT.Copy).then_inc(conv_high, 1)

                def values_high_part(t, r, c):
                    act.wait_ge(attn_in[c], 32 * (r + 1))
                    if live(t - 2):
                        act.wait_ge(out_acc, 2 * (t - 1))
                    nc.scalar.activation(vals_hi[:, c], vals[:, c], ACT.Copy).then_inc(vals_high, 1)

                def step(r, c):
                    if live(at(r, c, 1)[0]):
                        conv_high_part(*at(r, c, 1))
                    if live(at(r, c, 3)[0]):
                        values_high_part(*at(r, c, 3))

                run_steps(act, step, FIRST, LOOP, ENDS, LAST)

            @block.vector
            def _(dve):
                dve.wait_ge(pad_zero, 1)
                nc.vector.tensor_copy(late.conv_pad[:, 7:7 + TAPS, :],
                                      late.conv_rows[:, :, :].rearrange("o i k -> o k i")).then_inc(padded, 1)
                for p in range(PH):
                    dve.wait_ge(wo_high, p + 1)
                    nc.vector.tensor_tensor(wo_lo[:, :, p * P:(p + 1) * P],
                                            wo_ps[p % 4][:, :].rearrange("p (a n) -> p a n", a=HP),
                                            wo_hi[:, :, p * P:(p + 1) * P].bitcast(F32),
                                            ALU.subtract).then_inc(wo_low, 1)

                def values_low_part(t, r, c):
                    dve.wait_ge(vals_high, t + 1)
                    nc.vector.tensor_tensor(vals_lo[:, c], vals[:, c], vals_hi[:, c].bitcast(F32),
                                            ALU.subtract).then_inc(vals_low, 1)
                    nc.vector.tensor_tensor(x_sb[:, c, :], x_sb[:, c, :], late.bo[:, :], ALU.add).then_inc(x_biased, 1)

                def add_x(t, r, c):
                    dve.wait_ge(x_biased, t + 1)
                    if live(t - 2):
                        dve.wait_ge(x1_stored[c], 16 * r)
                    x_phases = x_sb[:, c, :].rearrange("p (j q) -> p q j", q=PH)
                    for b in range(2):
                        part = slice(H4 * b, H4 * b + H4)
                        dve.wait_ge(out_acc, 2 * t + b + 1)
                        nc.vector.tensor_tensor(x1[:, c, part, :], out_ps[b][:, :].rearrange("p (q j) -> p q j", j=NJ),
                                                x_phases[:, part, :], ALU.add).then_inc(x1_ready, 1)

                def add_conv_bias(t, r, c):
                    dve.wait_ge(convb_in[c], 16 * (r + 1))
                    for b in range(2):
                        part = slice(4 * b, 4 * b + 4)
                        dve.wait_ge(conv_acc, 2 * t + b + 1)
                        if live(t - 1):
                            dve.wait_ge(conv_low, 2 * t + b - 1)
                        nc.vector.tensor_tensor(conv[:, :, part].rearrange("p q g o -> p g q o"),
                                                conv_ps[b][:, :].rearrange("p (g q o) -> p g q o", g=4, q=PH),
                                                convb_sb[:, c, part, :].unsqueeze(2).to_broadcast([P, 4, PH, GC]),
                                                ALU.add).then_inc(conv_added, 1)

                def finish(t, r, c):
                    dve.wait_ge(x1_in[c], 16 * (r + 1))
                    if live(t - 2):
                        dve.wait_ge(out_stored[c], 16 * r)
                    for b in range(2):
                        cols = slice(b * BANK, (b + 1) * BANK)
                        dve.wait_ge(ffn_acc, 2 * t + b + 1)
                        nc.vector.scalar_tensor_tensor(
                            out=result[:, c, cols].rearrange("p (j q) -> p j q", q=PH),
                            in0=ffn_ps[b][:, :].rearrange("p (j q) -> p j q", q=PH), scalar=late.scale[:, 0:1],
                            in1=x1_res[:, c, :, b * (NJ // 2):(b + 1) * (NJ // 2)].rearrange("p q j -> p j q"),
                            op0=ALU.mult, op1=ALU.add).then_inc(result_ready, 1)

                def step(r, c):
                    if live(at(r, c, 2)[0]):
                        add_x(*at(r, c, 2))
                    if live(at(r, c, 1)[0]):
                        add_conv_bias(*at(r, c, 1))
                    if live(at(r, c, 3)[0]):
                        values_low_part(*at(r, c, 3))
                    if live(at(r, c, 0)[0]):
                        finish(*at(r, c, 0))

                run_steps(dve, step, FIRST, LOOP, ENDS, LAST)

            @block.tensor
            def _(pe):
                for p in range(PH):
                    if p >= 4:
                        pe.wait_ge(wo_low, p - 3)
                    for a in range(HP):
                        last = pe.transpose(wo_ps[p % 4][:, a * P:(a + 1) * P], late.wo_rows[:, p, a * P:(a + 1) * P], ident[:, :])
                    last.then_inc(wo_turned, 1)
                pe.wait_ge(padded, 1)
                for d in range(2):
                    for q in range(PH):
                        first = 7 + PH * d - q
                        last = pe.transpose(spare_ps[d][:, q * SEQ:(q + 1) * SEQ],
                                            late.conv_pad[:, first:first + PH, :].rearrange("o k i -> o (k i)"),
                                            ident[0:SEQ, 0:SEQ])
                    last.then_inc(bands_turned, 1)
                pe.wait_ge(wo_low, PH)

                def project(t, r, c):
                    pe.wait_ge(vals_low, t + 1)
                    for b in range(2):
                        if live(t - 1):
                            pe.wait_ge(x1_ready, 2 * t + b - 1)
                        n = 0
                        for a in range(HP):
                            for v, w in ((vals_hi, wo_hi), (vals_hi, wo_lo), (vals_lo, wo_hi)):
                                last = pe.matmul(out_ps[b][:, :], v[:, c, a, :], w[:, a, b * BANK:(b + 1) * BANK],
                                                 start=(n == 0), stop=(n == 3 * HP - 1))
                                n += 1
                        last.then_inc(out_acc, 1)

                def convolve(t, r, c):
                    pe.wait_ge(win_in[c], 16 * PH * (r + 1))
                    if isinstance(t, int) and t == 0:
                        pe.wait_ge(bands_out, 2)
                    for g in range(BG):
                        if g % 4 == 0 and live(t - 1):
                            pe.wait_ge(conv_added, 2 * t + g // 4 - 1)
                        for d in range(2):
                            last = pe.matmul(conv_ps[g // 4][:, (g % 4) * P:(g % 4 + 1) * P],
                                             win[:, c, g, d:d + NJ], bands[:, d, g % GROUPS, :],
                                             start=(d == 0), stop=(d == 1))
                        if g % 4 == 3:
                            last.then_inc(conv_acc, 1)

                def feed(t, r, c):
                    if isinstance(t, int) and t == 0:
                        pe.wait_ge(signed, PH)
                    pe.wait_ge(conv_low, 2 * (t + 1))
                    for b in range(2):
                        if live(t - 1):
                            pe.wait_ge(result_ready, 2 * t + b - 1)
                        n = 0
                        for p in range(PH):
                            for m in (conv_hi, conv_lo):
                                last = pe.matmul(ffn_ps[b][:, :], m[:, c, p].rearrange("p g o -> p (g o)"), signs[:, p, b * BANK:(b + 1) * BANK],
                                                 start=(n == 0), stop=(n == 2 * PH - 1))
                                n += 1
                        last.then_inc(ffn_acc, 1)

                def step(r, c):
                    if live(at(r, c, 2)[0]):
                        project(*at(r, c, 2))
                    if live(at(r, c, 1)[0]):
                        convolve(*at(r, c, 1))
                    if live(at(r, c, 0)[0]):
                        feed(*at(r, c, 0))

                run_steps(pe, step, FIRST, LOOP, ENDS, LAST)


_INS = ['x', 'cond_128', 'fside_S_0', 'L0_cond_W0', 'L0_cond_b0', 'L0_cond_W1', 'L0_cond_b1', 'L0_cond_W2',
        'L0_cond_b2', 'L0_cond_weight', 'L0_cond_bias_k', 'L0_attn_w_qkv', 'L0_attn_b_qkv', 'L0_attn_w_o',
        'L0_attn_b_o', 'L0_cond2_weight', 'L0_cond2_c_weight', 'L0_ffn_kernel', 'L0_ffn_scale']


def kernel(**inputs):
    import numpy as _np
    import concourse.bacc as _bacc
    from concourse import mybir as _mybir
    from concourse.bass_utils import run_bass_kernel_spmd as _run

    nc = _bacc.Bacc("TRN2", target_bir_lowering=False, num_devices=1)
    arrays, args = {}, []
    for name in _INS:
        a = _np.ascontiguousarray(inputs[name])
        if name == 'L0_ffn_scale':
            a = a.reshape(1, 1)
        arrays[f"in_{name}_dram"] = a
        args.append(nc.dram_tensor(f"in_{name}_dram", a.shape, _mybir.dt.from_np(a.dtype), kind="ExternalInput").ap())
    args.append(nc.dram_tensor("out_0_dram", (BATCH, SEQ, HID), F32, kind="ExternalOutput").ap())
    build(nc, *args)
    r = _run(nc, [arrays], core_ids=[0])
    return r.results[0]["out_0_dram"]
```

```python
from contextlib import ExitStack

import numpy as np

import concourse.bass as bass
from concourse import mybir

F32 = mybir.dt.float32
F32R = mybir.dt.float32r
BF16 = mybir.dt.bfloat16
U8 = mybir.dt.uint8
ALU = mybir.AluOpType
ACT = mybir.ActivationFunctionType
AX = mybir.AxisListType

P = 128
BATCH, SEQ, HID = 128, 64, 1024
PAIRS = BATCH // 2
QUADS = PAIRS // 2
HC = HID // P
HEADS, HEAD = 8, 64
PART = HEADS * HEAD
HP = HEADS // 2
QKV = 3 * PART
EXPERTS = 8
TAPS, PAD = 9, 4
GROUPS = 4
GC = SEQ // GROUPS
PH = P // GC
NJ = HID // PH
BG = 2 * GROUPS
BANK = 512
TURN = 32
MASKED = -10000.0


def live(t, steps=PAIRS):
    return not isinstance(t, int) or 0 <= t < steps


def at(r, c, d):
    r2, c2 = r + (c + d) // 2, (c + d) % 2
    return 2 * r2 + c2, r2, c2


def pair(q, e):
    return 2 * q + e, q, e


def run_steps(eng, step, first, loop_from, loop_to, last):
    for s in range(first, loop_from):
        step(s // 2, s % 2)
    with eng.Fori(loop_from // 2, loop_to // 2) as r:
        step(r, 0)
        step(r, 1)
    for s in range(loop_to, last + 1):
        step(s // 2, s % 2)


def build(nc, x, cond, fside, w0, b0, w1, b1, w2, b2, experts, bias_k,
          w_qkv, b_qkv, w_o, b_o, conv_w, ctx_w, ffn_k, ffn_scale, out):
    x_rows = x.rearrange("(t b) i h -> t (b i) h", b=2)
    out_rows = out.rearrange("(t b) i h -> t (b i) h", b=2)

    exp_d = nc.dram_tensor("exp_d", [PARTS, P, SEQ * SEQ // OG], BF16, kind="Internal").ap()
    mix_d = nc.dram_tensor("mix_d", [BATCH, SEQ, SEQ], F32, kind="Internal").ap()
    aggb_d = nc.dram_tensor("aggb_d", [PAIRS, 1, 2 * SEQ], F32, kind="Internal").ap()
    convb_d = nc.dram_tensor("convb_d", [PAIRS, 1, 2 * SEQ], F32, kind="Internal").ap()
    vals_d = nc.dram_tensor("vals_d", [PAIRS, P, HP * P], F32, kind="Internal").ap()
    x1_d = nc.dram_tensor("x1_d", [PAIRS, P, HID], F32, kind="Internal").ap()

    with ExitStack() as whole:
        def sb(name, shape, dt=F32):
            return whole.enter_context(nc.sbuf_tensor(name, shape, dt))

        ident = sb("ident", [P, P])
        with ExitStack() as setup:
            setup_tiles = setup_tensors(nc, setup)
        late = Late()
        late.wo_rows = sb("wo_rows", [P, PH, PART])
        late.kernel_u8 = sb("kernel_u8", [P, PH, HID], U8)
        late.conv_rows = sb("conv_rows", [SEQ, GC, TAPS])
        late.bo = sb("bo_sb", [P, HID])
        late.scale = sb("scale_sb", [P, 1])
        late.conv_pad = sb("conv_pad", [SEQ, CK, GC])
        late.conv = sb("conv", [P, PH, BG, GC])
        with ExitStack() as weights:
            w_hi = weights.enter_context(nc.sbuf_tensor("w_hi", [P, HC, QKV], F32R))
            w_lo = weights.enter_context(nc.sbuf_tensor("w_lo", [P, HC, QKV], F32R))
        late.wo_hi = sb("wo_hi", [P, HP, HID], F32R)
        late.wo_lo = sb("wo_lo", [P, HP, HID], F32R)
        late.bands_hi = sb("bands_hi", [P, 2, GROUPS, P], F32R)
        late.bands_lo = sb("bands_lo", [P, 2, GROUPS, P], F32R)
        late.vals = sb("vals_in", [P, 2, HP, P])
        late.x_sb = sb("x_res", [P, 2, HID])
        attend(nc, x_rows, cond, fside, w0, b0, w1, b1, w2, b2, experts, bias_k, ctx_w, w_qkv, b_qkv,
               w_o, b_o, conv_w, ffn_k, ffn_scale, ident, setup_tiles, late, w_hi, w_lo, exp_d, mix_d, aggb_d, convb_d, vals_d)
        feed_forward(nc, x_rows, ident, late, convb_d, vals_d, x1_d, out_rows)


class Late:
    pass


class Setup:
    pass


CK = 24
FT = QKV // P
WB = 7
OWN = 1
MIX_SLOTS = 4
EARLY = 9
PARTS = 3
KS = PARTS * PARTS * EXPERTS
OG = P // EXPERTS
MIXES = SEQ * SEQ // BANK


def setup_tensors(nc, stack):
    def sb(name, shape, dt=F32):
        return stack.enter_context(nc.sbuf_tensor(name, shape, dt))

    s = Setup()
    s.tri = sb("tri", [P, P])
    s.cond = sb("cond_sb", [BATCH, P])
    s.w0 = sb("w0_sb", [P, P])
    s.w1 = sb("w1_sb", [P, P])
    s.w2 = sb("w2_sb", [P, EXPERTS])
    s.b0 = sb("b0_sb", [P, 1])
    s.b1 = sb("b1_sb", [P, 1])
    s.b2 = sb("b2_sb", [BATCH, EXPERTS])
    s.bias_k = sb("bk_sb", [EXPERTS, SEQ])
    s.ctx_w = sb("ctxw_sb", [SEQ, P])
    s.fside = sb("fside_sb", [BATCH, SEQ])
    s.experts = sb("exp_w", [P, SEQ * SEQ // OG])
    s.exp_rest = sb("exp_rest", [P, SEQ * SEQ // OG])
    s.exp_split = sb("exp_split", [P, PARTS, SEQ * SEQ // OG], BF16)
    s.exp_parts = sb("exp_parts", [KS, SEQ, SEQ], BF16)
    s.w_rows = sb("w_rows", [P, OWN, HID])
    s.cond_t = sb("cond_t", [P, BATCH])
    s.ctxw_t = sb("ctxw_t", [P, SEQ])
    s.h1 = sb("h1", [P, BATCH])
    s.h2 = sb("h2", [P, BATCH])
    s.logits = sb("logits", [BATCH, EXPERTS])
    s.neg_max = sb("neg_max", [BATCH, 1])
    s.att_sum = sb("att_sum", [BATCH, 1])
    s.att_inv = sb("att_inv", [BATCH, 1])
    s.att_e = sb("att_e", [BATCH, EXPERTS])
    s.att = sb("att", [BATCH, EXPERTS])
    s.att_split = sb("att_split", [BATCH, 2, EXPERTS], BF16)
    s.att_rest = sb("att_rest", [BATCH, EXPERTS])
    s.att_parts = sb("att_parts", [BATCH, PARTS, PARTS, EXPERTS])
    s.att_t = sb("att_t", [EXPERTS, BATCH])
    s.att_parts_t = sb("att_parts_t", [KS, BATCH], BF16)
    s.aggb = sb("aggb", [BATCH, SEQ])
    s.convb = sb("convb", [BATCH, SEQ])
    s.mix = sb("mix", [BATCH, MIX_SLOTS, BANK])
    return s


def attend(nc, x_rows, cond, fside, w0, b0, w1, b1, w2, b2, experts, bias_k, ctx_w, w_qkv, b_qkv,
           w_o, b_o, conv_w, ffn_k, ffn_scale, ident, st, late, w_hi, w_lo, exp_d, mix_d, aggb_d, convb_d, vals_d):
    with ExitStack() as ctx:
        def sb(name, shape, dt=F32):
            return ctx.enter_context(nc.sbuf_tensor(name, shape, dt))

        def bank(name):
            return ctx.enter_context(nc.psum_tensor(name, [P, BANK], F32))

        def sem(name):
            return ctx.enter_context(nc.semaphore(name))

        sb("weights_rest", [P, 2 * HC * QKV - (2 * HP * HID + 4 * GROUPS * P + 2 * HP * P + 2 * HID)])
        mask = sb("mask", [P, SEQ])
        masked = sb("masked", [P, SEQ])
        qk_bias = sb("qk_bias", [P, 2 * HP])
        v_bias = sb("v_bias", [P, PART])
        x_sb = sb("x_sb", [P, 2, HID])
        mix_sb = sb("mix_sb", [P, 2, P])
        aggb_sb = sb("aggb_sb", [P, 2, P])
        y_sum = sb("y_sum", [P, HC, P])
        y_hi = sb("y_hi", [P, 2, HC, 2 * P], F32R)
        y_lo = sb("y_lo", [P, 2, HC, 2 * P], F32R)
        v_sb = sb("v_sb", [P, 2, PART])
        qk_t = sb("qk_t", [P, 2 * HP, 2 * P])
        scores = sb("scores", [P, HEADS, SEQ])
        row_max = sb("row_max", [P, HEADS])
        exps = sb("exps", [P, HEADS, SEQ])
        row_sum = sb("row_sum", [P, HEADS])
        row_inv = sb("row_inv", [P, HEADS])
        probs = sb("probs", [P, HEADS, SEQ])
        probs_t = sb("probs_t", [P, HEADS, P])
        vals = sb("vals", [P, 2, HP, P])

        qkv_ps = [bank("qkv_ps0"), bank("qkv_ps1")]
        y_ps = [bank("y_ps0"), bank("y_ps1")]
        score_ps = [bank("score_ps0"), bank("score_ps1")]
        vals_ps = [bank("vals_ps0"), bank("vals_ps1")]

        inputs_in = [sem("inputs_in0"), sem("inputs_in1")]
        bias_in, cleared = sem("bias_in"), sem("cleared")
        y_acc, y_added, y_high, y_low = sem("y_acc"), sem("y_added"), sem("y_high"), sem("y_low")
        qkv_acc, qkv_out = sem("qkv_acc"), sem("qkv_out")
        scores_acc, scores_cut, scores_masked = sem("scores_acc"), sem("scores_cut"), sem("scores_masked")
        maxed, shifted, exped, summed, inverted = (sem("maxed"), sem("shifted"), sem("exped"), sem("summed"),
                                                   sem("inverted"))
        probs_ready, probs_turned = sem("probs_ready"), sem("probs_turned")
        vals_acc, vals_out = sem("vals_acc"), sem("vals_out")
        vals_stored = [sem("vals_stored0"), sem("vals_stored1")]

        FIRST, LOOP, ENDS, LAST = -1, 2, QUADS - 2, QUADS

        cond_in, w0_in, w1_in, w2_in, biases_in, experts_in = (sem("cond_in"), sem("w0_in"), sem("w1_in"), sem("w2_in"),
                                                               sem("biases_in"), sem("experts_in"))
        experts_split, parts_stored, parts_in = sem("experts_split"), sem("parts_stored"), sem("parts_in")
        rows_in = [sem(f"rows_in{n}") for n in range(WB)]
        zeroed, consts, masks = sem("zeroed"), sem("consts"), sem("masks")
        chain_pe, chain_act, chain_dve = sem("chain_pe"), sem("chain_act"), sem("chain_dve")
        mix_acc, mix_out = sem("mix_acc"), [sem("mix_out0"), sem("mix_out1")]
        mix_stored = [sem(f"mix_stored{n}") for n in range(MIX_SLOTS)]
        biases_stored, late_in = sem("biases_stored"), sem("late_in")
        attn_first = sem("attn_first")
        wo_turned, wo_high, wo_low = sem("wo_turned"), sem("wo_high"), sem("wo_low")
        pad_zero, padded = sem("pad_zero"), sem("padded")
        bands_turned, bands_out = sem("bands_turned"), sem("bands_out")
        wo_ps = qkv_ps
        wt_acc, wt_hi, wt_lo = sem("wt_acc"), sem("wt_hi"), sem("wt_lo")
        wt_ps = score_ps + vals_ps
        mix_ps = [y_ps[0], y_ps[1]]
        w_rows = [st.w_rows[:, n, :] for n in range(OWN)] + [
            probs_t[:, :, :].rearrange("p a n -> p (a n)"), qk_t[:, 0:HP, :].rearrange("p a n -> p (a n)"),
            qk_t[:, HP:2 * HP, :].rearrange("p a n -> p (a n)"),
            v_sb[:, :, :].rearrange("p a n -> p (a n)"), vals[:, :, :, :].rearrange("p s a n -> p (s a n)"),
            y_sum[:, :, :].rearrange("p a n -> p (a n)")]

        def run_setup(gate, tile, step):
            gate(0)
            for f in range(FT):
                gate(f + 1)
                tile(f)
                if f == EARLY:
                    step(-1, 1)

        def mixes_at(k):
            return 2 * (k - 5) if 0 <= 2 * (k - 5) < MIXES else None

        def wt_out(w, n):
            f, half = n // 2, n % 2
            return w[:, 4 * half:4 * half + 4, f * P:(f + 1) * P]

        with nc.Block() as block:
            @block.sync
            def _(sp):
                def load_first_attention():
                    sp.wait_ge(qkv_acc, 6 * QUADS)
                    for n in range(2):
                        sp.wait_ge(vals_stored[n], 16)
                        sp.dma_start(late.vals[:, n, :, :].rearrange("p a n -> p (a n)"), vals_d[n]).then_inc(attn_first, 16)
                        sp.dma_start(late.x_sb[:, n, :], x_rows[n]).then_inc(attn_first, 16)

                def load_tile(f):
                    if f >= WB:
                        sp.wait_ge(wt_acc, 2 * (f - WB + 1))
                    sp.dma_start(w_rows[f % WB], w_qkv[f * P:(f + 1) * P, :]).then_inc(rows_in[f % WB], 16)

                def load_small(*loads):
                    for dst, src, done in loads:
                        sp.dma_start(dst, src).then_inc(done, 16)

                def store_mixed(n):
                    sp.wait_ge(mix_out[n % 2], n // 2 + 1)
                    sp.dma_start(mix_d.rearrange("b i o -> b (i o)")[:, n * BANK:(n + 1) * BANK],
                                 st.mix[:, n % MIX_SLOTS, :]).then_inc(mix_stored[n % MIX_SLOTS], 16)

                def load_late():
                    sp.wait_ge(wt_acc, 2 * FT)
                    for dst, src in ((late.wo_rows[:, :, :], w_o.rearrange("(j p) n -> j p n", p=PH)),
                                     (late.kernel_u8[:, :, :], ffn_k.rearrange("(j p) f -> j p f", p=PH)),
                                     (late.conv_rows[:, :, :], conv_w),
                                     (late.scale[:, :], ffn_scale.to_broadcast([P, 1])),
                                     (late.bo[:, :], b_o.rearrange("(a n) -> a n", a=1).to_broadcast([P, HID]))):
                        sp.dma_start(dst, src).then_inc(late_in, 16)

                def load_x(t, r, c):
                    if live(t - 2):
                        sp.wait_ge(y_added, 2 * (t - 1))
                    sp.dma_start(x_sb[:, c, :], x_rows[t]).then_inc(inputs_in[c], 16)

                def load_mix(t, r, c):
                    for b in range(2):
                        half = slice(SEQ * b, SEQ * b + SEQ)
                        sp.dma_start(mix_sb[half, c, half], mix_pairs[t, half, :]).then_inc(inputs_in[c], 16)
                    sp.dma_start(aggb_sb[:, c, :], aggb_d[t].to_broadcast([P, P])).then_inc(inputs_in[c], 16)

                def store(t, r, c):
                    sp.wait_ge(vals_out, t + 1)
                    sp.dma_start(vals_d[t], vals[:, c, :, :].rearrange("p a n -> p (a n)")).then_inc(vals_stored[c], 16)

                def step(r, c):
                    q = at(r, c, 0)[0]
                    for e in range(2):
                        if live(q + 2, QUADS):
                            load_x(*pair(q + 2, e))
                            load_mix(*pair(q + 2, e))
                        if live(q - 1, QUADS):
                            store(*pair(q - 1, e))
                        if isinstance(q, int) and q == QUADS and e == 0:
                            load_first_attention()
                    if isinstance(q, int) and q == 0:
                        load_late()

                mix_pairs = mix_d.rearrange("(t b) i o -> t (b i) o", b=2)
                load_small((st.cond[:, :], cond, cond_in),
                           (st.experts[:, :], experts.rearrange("k (g o) i a -> (k g) (o i a)", g=OG), experts_in),
                           (st.w0[:, :], w0, w0_in),
                           (st.b0[:, :], b0.rearrange("(p a) -> p a", a=1), w0_in))
                load_tile(0)
                load_small((st.w1[:, :], w1, w1_in),
                           (st.b1[:, :], b1.rearrange("(p a) -> p a", a=1), w1_in),
                           (st.w2[:, :], w2, w2_in),
                           (st.b2[:, :], b2.rearrange("(a k) -> a k", a=1).to_broadcast([BATCH, EXPERTS]), w2_in))
                load_tile(1)
                for part in range(PARTS):
                    sp.wait_ge(experts_split, (1, 3, 4)[part])
                    sp.dma_start(exp_d[part], st.exp_split[:, part, :]).then_inc(parts_stored, 16)
                load_small((st.ctx_w[:, :], ctx_w, biases_in),
                           (st.bias_k[:, :], bias_k, biases_in),
                           (st.fside[:, :], fside.rearrange("(a k) -> a k", a=1).to_broadcast([BATCH, SEQ]), biases_in))
                load_tile(2)
                sp.wait_ge(parts_stored, 16 * PARTS)
                for part in range(PARTS):
                    sp.dma_start(st.exp_parts[part * KS // PARTS:(part + 1) * KS // PARTS, :, :].rearrange("k o i -> k (o i)"),
                                 exp_d.rearrange("h (k g) x -> (h k) (g x)", g=OG)).then_inc(parts_in, 16)
                for f in range(3, 8):
                    load_tile(f)
                for n in range(0, MIXES, 2):
                    store_mixed(n)
                    store_mixed(n + 1)
                    if n == 2:
                        sp.wait_ge(chain_dve, 16)
                        sp.dma_start(aggb_d.rearrange("t a (b o) -> (t a b) o", b=2), st.aggb[:, :]).then_inc(biases_stored, 16)
                        sp.dma_start(convb_d.rearrange("t a (b o) -> (t a b) o", b=2), st.convb[:, :]).then_inc(biases_stored, 16)
                        load_x(0, 0, 0)
                    if n < 4:
                        load_tile(8 + n // 2)
                sp.wait_ge(cleared, 2)
                sp.wait_ge(biases_stored, 32)
                for n in range(MIX_SLOTS):
                    sp.wait_ge(mix_stored[n], 16 * (MIXES // MIX_SLOTS))
                load_mix(0, 0, 0)
                load_x(1, 0, 1)
                load_tile(10)
                load_tile(11)
                load_mix(1, 0, 1)
                load_small(*[(qk_bias[:, n:n + 1], b_qkv[n * P:(n + 1) * P].rearrange("(p a) -> p a", a=1), bias_in)
                             for n in range(2 * HP)],
                           (v_bias[:, :], b_qkv[2 * PART:].rearrange("(a n) -> a n", a=1).to_broadcast([P, PART]), bias_in))
                run_steps(sp, step, FIRST, LOOP, ENDS, LAST)
                sp.wait_ge(late_in, 80)
                sp.wait_ge(attn_first, 64)
                for c in range(2):
                    sp.wait_ge(vals_stored[c], 16 * (PAIRS // 2))

            @block.gpsimd
            def _(pool):
                nc.gpsimd.memset(ident[:, :], 0.0).then_inc(zeroed, 1)
                nc.gpsimd.memset(st.tri[:, :], 1.0).then_inc(zeroed, 1)
                pool.wait_ge(zeroed, 2)
                nc.gpsimd.affine_select(out=ident[:, :], in_=ident[:, :], compare_op=ALU.not_equal, fill=1.0,
                                        base=0, pattern=[[-1, P]], channel_multiplier=1).then_inc(consts, 1)
                nc.gpsimd.affine_select(out=st.tri[:, :], in_=st.tri[:, :], compare_op=ALU.is_ge, fill=0.0,
                                        base=0, pattern=[[-1, P]], channel_multiplier=1).then_inc(consts, 1)
                nc.gpsimd.memset(mix_sb[:, 0, :], 0.0).then_inc(cleared, 1)
                nc.gpsimd.memset(mix_sb[:, 1, :], 0.0).then_inc(cleared, 1)

                def add_masked(t, r, c):
                    pool.wait_ge(scores_cut, t + 1)
                    nc.gpsimd.tensor_tensor(scores[:, :, :], scores[:, :, :],
                                            masked[:, :].unsqueeze(1).to_broadcast([P, HEADS, SEQ]),
                                            ALU.add).then_inc(scores_masked, 1)

                def low_part(t, r, c, slot):
                    for b in range(2):
                        chunks = slice(4 * b, 4 * b + 4)
                        pool.wait_ge(y_high, 2 * t + b + 1)
                        nc.gpsimd.tensor_tensor(y_lo[:, slot, chunks, c * P:(c + 1) * P], y_sum[:, chunks, :],
                                                y_hi[:, slot, chunks, c * P:(c + 1) * P].bitcast(F32),
                                                ALU.subtract).then_inc(y_low, 1)

                def step(r, c):
                    q = at(r, c, 0)[0]
                    for e in range(2):
                        if live(q - 1, QUADS):
                            add_masked(*pair(q - 1, e))
                        if live(q + 1, QUADS):
                            low_part(*pair(q + 1, e), at(r, c, 1)[2])

                step(-1, 1)
                pool.wait_ge(wt_acc, 2 * FT)
                nc.gpsimd.memset(probs_t[:, :, :], 0.0).then_inc(cleared, 1)
                run_steps(pool, step, 0, LOOP, ENDS, LAST)
                nc.gpsimd.memset(late.conv_pad[:, :, :], 0.0).then_inc(pad_zero, 1)

            @block.scalar
            def _(act):
                def gate(k):
                    if k == 1:
                        act.wait_ge(chain_pe, 2)
                        nc.scalar.activation(st.h1[:, :], qkv_ps[1][:, 0:BATCH], ACT.Gelu,
                                             bias=st.b0[:, 0:1]).then_inc(chain_act, 1)
                    if k == 2:
                        act.wait_ge(chain_pe, 3)
                        nc.scalar.activation(st.h2[:, :], qkv_ps[0][:, 0:BATCH], ACT.Gelu,
                                             bias=st.b1[:, 0:1]).then_inc(chain_act, 1)
                    if k == 3:
                        act.wait_ge(chain_dve, 3)
                        nc.scalar.activation(st.att_e[:, :], st.logits[:, :], ACT.Exp, bias=st.neg_max[:, 0:1],
                                             accum_out=st.att_sum[:, 0:1]).then_inc(chain_act, 1)
                    if mixes_at(k) is not None:
                        n = mixes_at(k)
                        act.wait_ge(mix_acc, n + 1)
                        if n >= MIX_SLOTS:
                            act.wait_ge(mix_stored[n % MIX_SLOTS], 16 * (n // MIX_SLOTS))
                        nc.scalar.activation(st.mix[:, n % MIX_SLOTS, :], mix_ps[0][:, :], ACT.Copy).then_inc(mix_out[0], 1)

                def tile_high(f):
                    for n in (2 * f, 2 * f + 1):
                        act.wait_ge(wt_acc, n + 1)
                        nc.scalar.activation(wt_out(w_hi, n), wt_ps[n % 4][:, :].rearrange("p (q f) -> p q f", q=4),
                                             ACT.Copy).then_inc(wt_hi, 1)

                def values_out(t, r, c):
                    act.wait_ge(vals_acc, t + 1)
                    if live(t - 2):
                        act.wait_ge(vals_stored[c], 16 * r)
                    nc.scalar.activation(vals[:, c, :, :], vals_ps[c][:, :].rearrange("p (a n) -> p a n", a=HP),
                                         ACT.Copy).then_inc(vals_out, 1)

                def exponent(t, r, c):
                    act.wait_ge(shifted, t + 1)
                    if live(t - 1):
                        act.wait_ge(probs_ready, t)
                    nc.scalar.activation(exps[:, :, :], scores[:, :, :], ACT.Exp).then_inc(exped, 1)

                def high_part(t, r, c, slot):
                    if live(r - 2, QUADS):
                        act.wait_ge(qkv_acc, 6 * (r - 1))
                    for b in range(2):
                        chunks = slice(4 * b, 4 * b + 4)
                        act.wait_ge(y_added, 2 * t + b + 1)
                        nc.scalar.activation(y_hi[:, slot, chunks, c * P:(c + 1) * P], y_sum[:, chunks, :], ACT.Copy).then_inc(y_high, 1)

                def wo_high_part(*phases):
                    for n in phases:
                        act.wait_ge(wo_turned, n + 1)
                        nc.scalar.activation(late.wo_hi[:, :, n * P:(n + 1) * P],
                                             wo_ps[n % 2][:, :].rearrange("p (a n) -> p a n", a=HP),
                                             ACT.Copy).then_inc(wo_high, 1)

                def step(r, c):
                    q = at(r, c, 0)[0]
                    ending = isinstance(q, int) and q == QUADS
                    if ending:
                        wo_high_part(0, 1)
                    if live(q - 1, QUADS):
                        exponent(*pair(q - 1, 0))
                    if ending:
                        wo_high_part(2, 3)
                    if live(q + 1, QUADS):
                        high_part(*pair(q + 1, 0), at(r, c, 1)[2])
                    if live(q - 1, QUADS):
                        exponent(*pair(q - 1, 1))
                        values_out(*pair(q - 1, 0))
                    if ending:
                        wo_high_part(4, 5)
                    if live(q + 1, QUADS):
                        high_part(*pair(q + 1, 1), at(r, c, 1)[2])
                    if live(q - 1, QUADS):
                        values_out(*pair(q - 1, 1))
                    if ending:
                        wo_high_part(6, 7)

                run_setup(gate, tile_high, step)
                run_steps(act, step, 0, LOOP, ENDS, LAST)
                for d in range(2):
                    act.wait_ge(bands_turned, d + 1)
                    nc.scalar.activation(late.bands_hi[:, d, :, :].rearrange("p g (q o) -> p q g o", q=PH),
                                         wo_ps[(PH + d) % 2][:, :].rearrange("p (q g o) -> p q g o", q=PH, g=GROUPS),
                                         ACT.Copy).then_inc(bands_out, 1)

            @block.vector
            def _(dve):
                dve.wait_ge(consts, 2)
                for b in range(2):
                    rows = slice(SEQ * b, SEQ * b + SEQ)
                    last = nc.vector.tensor_copy(mask[rows, :], st.tri[rows, rows])
                last.then_inc(masks, 1)
                dve.wait_ge(masks, 1)
                nc.vector.tensor_scalar(masked[:, :], mask[:, :], -MASKED, MASKED, ALU.mult, ALU.add).then_inc(masks, 1)

                def gate(k):
                    if k == 0:
                        dve.wait_ge(chain_pe, 1)
                        nc.vector.tensor_copy(st.cond_t[:, :], qkv_ps[0][:, 0:BATCH]).then_inc(chain_dve, 1)
                        dve.wait_ge(experts_in, 16)
                        nc.vector.tensor_copy(st.exp_split[:, 0, :], st.experts[:, :]).then_inc(experts_split, 1)
                        dve.wait_ge(experts_split, 1)
                        nc.vector.tensor_tensor(st.exp_rest[:, :], st.experts[:, :], st.exp_split[:, 0, :],
                                                ALU.subtract).then_inc(experts_split, 1)
                        dve.wait_ge(experts_split, 2)
                        nc.vector.tensor_copy(st.exp_split[:, 1, :], st.exp_rest[:, :]).then_inc(experts_split, 1)
                        dve.wait_ge(experts_split, 3)
                        nc.vector.tensor_tensor(st.exp_split[:, 2, :], st.exp_rest[:, :], st.exp_split[:, 1, :],
                                                ALU.subtract).then_inc(experts_split, 1)
                    if k == 3:
                        dve.wait_ge(chain_pe, 4)
                        nc.vector.tensor_tensor(st.logits[:, :], qkv_ps[1][:, 0:EXPERTS], st.b2[:, :],
                                                ALU.add).then_inc(chain_dve, 1)
                        dve.wait_ge(chain_dve, 2)
                        nc.vector.tensor_reduce(st.neg_max[:, :], st.logits[:, :], AX.X, ALU.max,
                                                negate=True).then_inc(chain_dve, 1)
                        dve.wait_ge(chain_act, 3)
                        nc.vector.reciprocal(st.att_inv[:, :], st.att_sum[:, :]).then_inc(chain_dve, 1)
                        dve.wait_ge(chain_dve, 4)
                        nc.vector.tensor_scalar(st.att[:, :], st.att_e[:, :], st.att_inv[:, 0:1], None,
                                                ALU.mult).then_inc(chain_dve, 1)
                        dve.wait_ge(chain_dve, 5)
                        nc.vector.tensor_copy(st.att_split[:, 0, :], st.att[:, :]).then_inc(chain_dve, 1)
                        dve.wait_ge(chain_dve, 6)
                        nc.vector.tensor_tensor(st.att_rest[:, :], st.att[:, :], st.att_split[:, 0, :],
                                                ALU.subtract).then_inc(chain_dve, 1)
                        dve.wait_ge(chain_dve, 7)
                        nc.vector.tensor_copy(st.att_split[:, 1, :], st.att_rest[:, :]).then_inc(chain_dve, 1)
                        dve.wait_ge(chain_dve, 8)
                        for part in range(2):
                            nc.vector.tensor_copy(st.att_parts[:, part, :, :],
                                                  st.att_split[:, part, :].unsqueeze(1).to_broadcast([BATCH, PARTS, EXPERTS])
                                                  ).then_inc(chain_dve, 1)
                        nc.vector.tensor_tensor(st.att_parts[:, 2, :, :],
                                                st.att_rest[:, :].unsqueeze(1).to_broadcast([BATCH, PARTS, EXPERTS]),
                                                st.att_split[:, 1, :].unsqueeze(1).to_broadcast([BATCH, PARTS, EXPERTS]),
                                                ALU.subtract).then_inc(chain_dve, 1)
                    if k == 4:
                        dve.wait_ge(chain_pe, 5)
                        nc.vector.tensor_copy(st.att_parts_t[:, :], qkv_ps[0][0:KS, 0:BATCH]).then_inc(chain_dve, 1)
                        nc.vector.tensor_copy(st.att_t[:, :], qkv_ps[0][0:EXPERTS, P:P + BATCH]).then_inc(chain_dve, 1)
                        nc.vector.tensor_copy(st.ctxw_t[:, :], qkv_ps[0][:, 2 * P:2 * P + SEQ]).then_inc(chain_dve, 1)
                    if k == 6:
                        dve.wait_ge(chain_pe, 7)
                        nc.vector.tensor_copy(st.aggb[:, :], qkv_ps[1][:, 0:SEQ]).then_inc(chain_dve, 1)
                        nc.vector.tensor_tensor(st.convb[:, :], qkv_ps[0][:, 0:SEQ], st.fside[:, :],
                                                ALU.add).then_inc(chain_dve, 1)
                    if mixes_at(k) is not None:
                        n = mixes_at(k) + 1
                        dve.wait_ge(mix_acc, n + 1)
                        if n >= MIX_SLOTS:
                            dve.wait_ge(mix_stored[n % MIX_SLOTS], 16 * (n // MIX_SLOTS))
                        nc.vector.tensor_copy(st.mix[:, n % MIX_SLOTS, :], mix_ps[1][:, :]).then_inc(mix_out[1], 1)

                def tile_low(f):
                    for n in (2 * f, 2 * f + 1):
                        dve.wait_ge(wt_hi, n + 1)
                        nc.vector.tensor_tensor(wt_out(w_lo, n), wt_ps[n % 4][:, :].rearrange("p (q f) -> p q f", q=4),
                                                wt_out(w_hi, n).bitcast(F32), ALU.subtract).then_inc(wt_lo, 1)

                def qk_part_out(q, i):
                    if isinstance(q, int) and q == 0 and i == 0:
                        dve.wait_ge(bias_in, 16 * (2 * HP + 1))
                    dve.wait_ge(qkv_acc, 6 * q + i + 1)
                    if live(q - 1, QUADS):
                        dve.wait_ge(scores_acc, 2 * q)
                    nc.vector.tensor_tensor(qk_t[:, 2 * i:2 * i + 2, :],
                                            qkv_ps[i % 2][:, :].rearrange("p (a n) -> p a n", a=2),
                                            qk_bias[:, 2 * i:2 * i + 2].unsqueeze(2).to_broadcast([P, 2, 2 * P]),
                                            ALU.add).then_inc(qkv_out, 1)

                def v_out(t, q, e):
                    dve.wait_ge(qkv_acc, 6 * q + 4 + e + 1)
                    if live(t - 2):
                        dve.wait_ge(vals_acc, t - 1)
                    nc.vector.tensor_tensor(v_sb[:, e, :], qkv_ps[e][:, :], v_bias[:, :], ALU.add).then_inc(qkv_out, 1)

                def wo_low_part(*phases):
                    for n in phases:
                        dve.wait_ge(wo_high, n + 1)
                        nc.vector.tensor_tensor(late.wo_lo[:, :, n * P:(n + 1) * P],
                                                wo_ps[n % 2][:, :].rearrange("p (a n) -> p a n", a=HP),
                                                late.wo_hi[:, :, n * P:(n + 1) * P].bitcast(F32),
                                                ALU.subtract).then_inc(wo_low, 1)

                def softmax(t, r, c):
                    ending = isinstance(t, int) and t >= PAIRS - 2
                    dve.wait_ge(scores_acc, 2 * (r + 1))
                    if live(t - 1):
                        dve.wait_ge(exped, t)
                    for parity in range(2):
                        last = nc.vector.tensor_tensor(
                            scores[:, HP * parity:HP * parity + HP, :],
                            score_ps[parity][:, c * HP * SEQ:(c + 1) * HP * SEQ].rearrange("p (a f) -> p a f", a=HP),
                            mask[:, :].unsqueeze(1).to_broadcast([P, HP, SEQ]), ALU.mult)
                    last.then_inc(scores_cut, 1)
                    if ending:
                        wo_low_part(2 * c, 2 * c + 1)
                    dve.wait_ge(scores_masked, t + 1)
                    nc.vector.tensor_reduce(row_max[:, :], scores[:, :, :], AX.X, ALU.max).then_inc(maxed, 1)
                    dve.wait_ge(maxed, t + 1)
                    nc.vector.tensor_tensor(scores[:, :, :], scores[:, :, :],
                                            row_max[:, :].unsqueeze(2).to_broadcast([P, HEADS, SEQ]),
                                            ALU.subtract).then_inc(shifted, 1)
                    dve.wait_ge(exped, t + 1)
                    nc.vector.tensor_reduce(row_sum[:, :], exps[:, :, :], AX.X, ALU.add).then_inc(summed, 1)
                    dve.wait_ge(summed, t + 1)
                    nc.vector.reciprocal(row_inv[:, :], row_sum[:, :]).then_inc(inverted, 1)

                def normalise(t, r, c):
                    dve.wait_ge(inverted, t + 1)
                    if live(t - 1):
                        dve.wait_ge(probs_turned, t)
                    nc.vector.tensor_tensor(probs[:, :, :], exps[:, :, :],
                                            row_inv[:, :].unsqueeze(2).to_broadcast([P, HEADS, SEQ]),
                                            ALU.mult).then_inc(probs_ready, 1)

                def turn_probs(t, r, c):
                    dve.wait_ge(probs_ready, t + 1)
                    if live(t - 1):
                        dve.wait_ge(vals_acc, t)
                    for b in range(2):
                        for i in range(2):
                            for j in range(2):
                                here, there = SEQ * b + TURN * i, SEQ * b + TURN * j
                                last = nc.vector.transpose(probs_t[there:there + TURN, :, here:here + TURN],
                                                           probs[here:here + TURN, :, TURN * j:TURN * (j + 1)])
                    last.then_inc(probs_turned, 1)

                def add_bias(t, r, c):
                    for b in range(2):
                        chunks = slice(4 * b, 4 * b + 4)
                        dve.wait_ge(y_acc, 2 * t + b + 1)
                        if live(t - 1):
                            dve.wait_ge(y_low, 2 * t + b - 1)
                        nc.vector.tensor_tensor(y_sum[:, chunks, :], y_ps[b][:, :].rearrange("p (a n) -> p a n", a=4),
                                                aggb_sb[:, c, :].unsqueeze(1).to_broadcast([P, 4, P]),
                                                ALU.add).then_inc(y_added, 1)

                def step(r, c):
                    q = at(r, c, 0)[0]
                    if live(q, QUADS):
                        qk_part_out(q, 0)
                    if isinstance(q, int) and q == 1:
                        dve.wait_ge(cleared, 3)
                    if live(q - 1, QUADS):
                        softmax(*pair(q - 1, 0))
                        normalise(*pair(q - 1, 0))
                        turn_probs(*pair(q - 1, 0))
                    if live(q, QUADS):
                        qk_part_out(q, 1)
                    if live(q + 1, QUADS):
                        add_bias(*pair(q + 1, 0))
                    if live(q - 1, QUADS):
                        softmax(*pair(q - 1, 1))
                    if live(q, QUADS):
                        qk_part_out(q, 2)
                    if live(q - 1, QUADS):
                        normalise(*pair(q - 1, 1))
                    if live(q, QUADS):
                        qk_part_out(q, 3)
                    if live(q - 1, QUADS):
                        turn_probs(*pair(q - 1, 1))
                    if live(q + 1, QUADS):
                        add_bias(*pair(q + 1, 1))
                    if live(q, QUADS):
                        v_out(*pair(q, 0))
                        v_out(*pair(q, 1))

                run_setup(gate, tile_low, step)
                run_steps(dve, step, 0, LOOP, ENDS, LAST)
                dve.wait_ge(pad_zero, 1)
                dve.wait_ge(late_in, 80)
                nc.vector.tensor_copy(late.conv_pad[:, 7:7 + TAPS, :],
                                      late.conv_rows[:, :, :].rearrange("o i k -> o k i")).then_inc(padded, 1)
                wo_low_part(4, 5, 6, 7)
                for d in range(2):
                    dve.wait_ge(bands_out, d + 1)
                    nc.vector.tensor_tensor(late.bands_lo[:, d, :, :].rearrange("p g (q o) -> p q g o", q=PH),
                                            wo_ps[(PH + d) % 2][:, :].rearrange("p (q g o) -> p q g o", q=PH, g=GROUPS),
                                            late.bands_hi[:, d, :, :].rearrange("p g (q o) -> p q g o", q=PH).bitcast(F32),
                                            ALU.subtract)

            @block.tensor
            def _(pe):
                def gate(k):
                    if k == 0:
                        pe.wait_ge(cond_in, 16)
                        pe.transpose(qkv_ps[0][:, 0:BATCH], st.cond[:, :], ident[:, :]).then_inc(chain_pe, 1)
                    if k == 1:
                        pe.wait_ge(w0_in, 32)
                        pe.wait_ge(chain_dve, 1)
                        pe.matmul(qkv_ps[1][:, 0:BATCH], st.w0[:, :], st.cond_t[:, :], start=True, stop=True).then_inc(chain_pe, 1)
                    if k == 2:
                        pe.wait_ge(w1_in, 32)
                        pe.wait_ge(chain_act, 1)
                        pe.matmul(qkv_ps[0][:, 0:BATCH], st.w1[:, :], st.h1[:, :], start=True, stop=True).then_inc(chain_pe, 1)
                    if k == 3:
                        pe.wait_ge(w2_in, 32)
                        pe.wait_ge(chain_act, 2)
                        pe.matmul(qkv_ps[1][:, 0:EXPERTS], st.h2[:, :], st.w2[:, :], start=True, stop=True).then_inc(chain_pe, 1)
                    if k == 4:
                        pe.wait_ge(chain_dve, 11)
                        pe.transpose(qkv_ps[0][0:KS, 0:BATCH], st.att_parts[:, :, :].rearrange("b a e k -> b (a e k)"), ident[:, :])
                        pe.transpose(qkv_ps[0][0:EXPERTS, P:P + BATCH], st.att[:, :], ident[:, :])
                        pe.wait_ge(biases_in, 48)
                        pe.transpose(qkv_ps[0][:, 2 * P:2 * P + SEQ], st.ctx_w[:, :], ident[0:SEQ, 0:SEQ]).then_inc(chain_pe, 1)
                    if k == 6:
                        pe.matmul(qkv_ps[1][:, 0:SEQ], st.att_t[:, :], st.bias_k[:, :], start=True, stop=True).then_inc(chain_pe, 1)
                        pe.matmul(qkv_ps[0][:, 0:SEQ], st.cond_t[:, :], st.ctxw_t[:, :], start=True, stop=True).then_inc(chain_pe, 1)
                    if mixes_at(k) is not None:
                        if k == 5:
                            pe.wait_ge(parts_in, 16 * PARTS)
                            pe.wait_ge(chain_dve, 14)
                        ins = BANK // SEQ
                        for n in (mixes_at(k), mixes_at(k) + 1):
                            if n >= 2:
                                pe.wait_ge(mix_out[n % 2], n // 2)
                            pe.matmul(mix_ps[n % 2][:, :], st.att_parts_t[:, :],
                                      st.exp_parts[:, :, n * ins:(n + 1) * ins].rearrange("k o i -> k i o"),
                                      start=True, stop=True).then_inc(mix_acc, 1)

                pe.wait_ge(consts, 1)
                def turn_tile(f):
                    pe.wait_ge(rows_in[f % WB], 16 * (f // WB + 1))
                    for n in (2 * f, 2 * f + 1):
                        if n >= 4:
                            pe.wait_ge(wt_lo, n - 3)
                        for q in range(4):
                            h = 4 * (n % 2) + q
                            last = pe.transpose(wt_ps[n % 4][:, q * P:(q + 1) * P],
                                                w_rows[f % WB][:, h * P:(h + 1) * P], ident[:, :])
                        last.then_inc(wt_acc, 1)

                def mix_x(t, r, c):
                    if isinstance(t, int) and t == 0:
                        for b in range(2):
                            pe.wait_ge(mix_out[b], MIXES // 2)
                    pe.wait_ge(inputs_in[c], 64 * (r + 1))
                    if live(t - 1):
                        pe.wait_ge(y_added, 2 * t)
                    for h in range(HC):
                        last = pe.matmul(y_ps[h // 4][:, (h % 4) * P:(h % 4 + 1) * P], x_sb[:, c, h * P:(h + 1) * P],
                                         mix_sb[:, c, :], start=True, stop=True)
                        if h % 4 == 3:
                            last.then_inc(y_acc, 1)

                def bank_ready(q, i):
                    if isinstance(q, int) and q == 0:
                        pe.wait_ge(wt_lo, min(4 * (i + 1), 2 * FT) if i < 4 else 2 * FT)
                        pe.wait_ge(chain_dve, 16)
                    if not isinstance(q, int) or 6 * q + i >= 2:
                        pe.wait_ge(qkv_out, 6 * q + i - 1)

                def qk_part(q, i, slot):
                    if i == 0:
                        pe.wait_ge(y_low, 4 * (q + 1))
                    bank_ready(q, i)
                    for half in range(2):
                        cols = slice((2 * i + half) * P, (2 * i + half + 1) * P)
                        n = 0
                        for h in range(HC):
                            for w, y in ((w_hi, y_hi), (w_hi, y_lo), (w_lo, y_hi)):
                                last = pe.matmul(qkv_ps[i % 2][:, half * 2 * P:(half + 1) * 2 * P], w[:, h, cols], y[:, slot, h, :],
                                                 start=(n == 0), stop=(n == 3 * HC - 1))
                                n += 1
                    last.then_inc(qkv_acc, 1)

                def v_part(q, e, slot):
                    bank_ready(q, 4 + e)
                    n = 0
                    for h in range(HC):
                        for y, w in ((y_hi, w_hi), (y_hi, w_lo), (y_lo, w_hi)):
                            last = pe.matmul(qkv_ps[e][:, :], y[:, slot, h, e * P:(e + 1) * P], w[:, h, 2 * PART:3 * PART],
                                             start=(n == 0), stop=(n == 3 * HC - 1))
                            n += 1
                    last.then_inc(qkv_acc, 1)

                def score(t, r, c):
                    pe.wait_ge(qkv_out, 6 * r + 4)
                    if live(t - 2):
                        pe.wait_ge(scores_cut, 2 * r)
                    pe.nop(nofuse=True)
                    for a in range(HP):
                        for b in range(2):
                            rows = slice(SEQ * b, SEQ * b + SEQ)
                            for parity in range(2):
                                head = slice(HEAD * parity, HEAD * parity + HEAD)
                                cols = slice(c * P + SEQ * b, c * P + SEQ * b + SEQ)
                                last = pe.matmul(score_ps[parity][rows, (c * HP + a) * SEQ:(c * HP + a + 1) * SEQ],
                                                 qk_t[head, a, cols], qk_t[head, HP + a, cols], start=True, stop=True)
                    last.then_inc(scores_acc, 1)

                def values(t, r, c):
                    pe.wait_ge(probs_turned, t + 1)
                    if live(t - 2):
                        pe.wait_ge(vals_out, t - 1)
                    pe.nop(nofuse=True)
                    for a in range(HP):
                        for parity in range(2):
                            head = 2 * a + parity
                            last = pe.matmul(vals_ps[c][HEAD * parity:HEAD * parity + HEAD, a * P:(a + 1) * P],
                                             v_sb[:, c, head * HEAD:(head + 1) * HEAD], probs_t[:, HP * parity + a, :],
                                             start=True, stop=True)
                    last.then_inc(vals_acc, 1)

                def turn_wo(*phases):
                    for n in phases:
                        if n == 0:
                            pe.wait_ge(late_in, 80)
                            pe.wait_ge(qkv_out, 6 * QUADS)
                        if n >= 2:
                            pe.wait_ge(wo_low, n - 1)
                        for a in range(HP):
                            last = pe.transpose(wo_ps[n % 2][:, a * P:(a + 1) * P], late.wo_rows[:, n, a * P:(a + 1) * P],
                                                ident[:, :])
                        last.then_inc(wo_turned, 1)

                def turn_bands():
                    pe.wait_ge(padded, 1)
                    for d in range(2):
                        pe.wait_ge(wo_low, PH + d - 1)
                        for q in range(PH):
                            first = 7 + PH * d - q
                            last = pe.transpose(wo_ps[(PH + d) % 2][:, q * SEQ:(q + 1) * SEQ],
                                                late.conv_pad[:, first:first + PH, :].rearrange("o k i -> o (k i)"),
                                                ident[0:SEQ, 0:SEQ])
                        last.then_inc(bands_turned, 1)

                def step(r, c):
                    q, _, slot = at(r, c, 0)
                    if live(q, QUADS):
                        qk_part(q, 0, slot)
                    if live(q - 1, QUADS):
                        score(*pair(q - 1, 0))
                        score(*pair(q - 1, 1))
                    if isinstance(q, int) and q == QUADS:
                        turn_wo(0, 1, 2, 3)
                    if live(q, QUADS):
                        qk_part(q, 1, slot)
                    if live(q + 1, QUADS):
                        mix_x(*pair(q + 1, 0))
                    if live(q, QUADS):
                        qk_part(q, 2, slot)
                    if live(q, QUADS):
                        qk_part(q, 3, slot)
                    if live(q - 1, QUADS):
                        values(*pair(q - 1, 0))
                    if isinstance(q, int) and q == QUADS:
                        turn_wo(4, 5)
                    if live(q + 1, QUADS):
                        mix_x(*pair(q + 1, 1))
                    if live(q, QUADS):
                        v_part(q, 0, slot)
                    if live(q - 1, QUADS):
                        values(*pair(q - 1, 1))
                    if live(q, QUADS):
                        v_part(q, 1, slot)

                run_setup(gate, turn_tile, step)
                run_steps(pe, step, 0, LOOP, ENDS, LAST)
                turn_wo(6, 7)
                turn_bands()


def feed_forward(nc, x_rows, ident, late, convb_d, vals_d, x1_d, out_rows):
    with ExitStack() as ctx:
        def sb(name, shape, dt=F32):
            return ctx.enter_context(nc.sbuf_tensor(name, shape, dt))

        def bank(name):
            return ctx.enter_context(nc.psum_tensor(name, [P, BANK], F32))

        def sem(name):
            return ctx.enter_context(nc.semaphore(name))

        wo_hi, wo_lo, bands_hi, bands_lo = late.wo_hi, late.wo_lo, late.bands_hi, late.bands_lo
        vals, x_sb = late.vals, late.x_sb
        conv = late.conv
        signs = sb("signs", [P, PH, HID], F32R)

        out_ps = [bank("out_ps0"), bank("out_ps1")]
        ffn_ps = [bank("ffn_ps0"), bank("ffn_ps1")]
        conv_ps = [bank("conv_ps0"), bank("conv_ps1")]

        vals_hi = sb("vals_hi", [P, 2, HP, P], F32R)
        vals_lo = sb("vals_lo", [P, 2, HP, P], F32R)
        x1 = sb("x1", [P, 2, PH, NJ])
        x1_res = sb("x1_res", [P, 2, PH, NJ])
        win = sb("win", [P, 2, BG, NJ + 1])
        win_hi = sb("win_hi", [P, 2, 2, GROUPS, NJ + 1], F32R)
        win_lo = sb("win_lo", [P, 2, 2, GROUPS, NJ + 1], F32R)
        conv_sum = sb("conv_sum", [P, 2, GROUPS, P])
        convb_sb = sb("convb_sb", [P, 2, BG, GC])
        conv_hi = sb("conv_hi", [P, 2, PH, BG, GC], F32R)
        conv_lo = sb("conv_lo", [P, 2, PH, BG, GC], F32R)
        result = sb("result", [P, 2, HID])

        attn_in = [sem("attn_in0"), sem("attn_in1")]
        convb_in = [sem("convb_in0"), sem("convb_in1")]
        x1_stored = [sem("x1_stored0"), sem("x1_stored1")]
        win_in = [sem("win_in0"), sem("win_in1")]
        x1_in = [sem("x1_in0"), sem("x1_in1")]
        out_stored = [sem("out_stored0"), sem("out_stored1")]
        edges, signed = sem("edges"), sem("signed")
        vals_high, vals_low = sem("vals_high"), sem("vals_low")
        x_biased = sem("x_biased")
        out_acc, x1_ready = sem("out_acc"), sem("x1_ready")
        win_high, win_low, conv_turned = sem("win_high"), sem("win_low"), sem("conv_turned")
        conv_acc, conv_added, conv_high, conv_low = sem("conv_acc"), sem("conv_added"), sem("conv_high"), sem("conv_low")
        ffn_acc, result_ready = sem("ffn_acc"), sem("result_ready")

        FIRST, LOOP, ENDS, LAST = -4, 2, PAIRS - 6, PAIRS - 1
        H4 = PH // 2

        with nc.Block() as block:
            @block.sync
            def _(sp):
                def load_attention(t, r, c):
                    sp.wait_ge(x1_ready, 2 * (t - 1))
                    sp.dma_start(vals[:, c, :, :].rearrange("p a n -> p (a n)"), vals_d[t]).then_inc(attn_in[c], 16)
                    sp.dma_start(x_sb[:, c, :], x_rows[t]).then_inc(attn_in[c], 16)

                def store_x1(t, r, c):
                    sp.wait_ge(x1_ready, 2 * (t + 1))
                    sp.dma_start(x1_d[t], x1[:, c, :, :].rearrange("p q j -> p (q j)")).then_inc(x1_stored[c], 16)

                def load_window(t, r, c):
                    if live(t - 2):
                        sp.wait_ge(win_low, t - 1)
                    sp.wait_ge(x1_stored[c], 16 * (r + 1))
                    phases = x1_d[t].rearrange("(g i) (p j) -> p i g j", i=GC, p=PH)
                    for p in range(PH):
                        row, shift = (p + PAD) % PH, (p + PAD) // PH
                        sp.dma_start(win[row * GC:(row + 1) * GC, c, :, shift:shift + NJ],
                                     phases[p]).then_inc(win_in[c], 16)

                def load_conv_bias(t, r, c):
                    if live(t - 2):
                        sp.wait_ge(conv_added, 2 * (t - 1))
                    sp.dma_start(convb_sb[:, c, :, :].rearrange("p g o -> p (g o)"),
                                 convb_d[t].to_broadcast([P, P])).then_inc(convb_in[c], 16)

                def load_x1(t, r, c):
                    sp.wait_ge(x1_stored[c], 16 * (r + 1))
                    if live(t - 2):
                        sp.wait_ge(result_ready, 2 * (t - 1))
                    sp.dma_start(x1_res[:, c, :, :].rearrange("p q j -> p (q j)"), x1_d[t]).then_inc(x1_in[c], 16)

                def store_result(t, r, c):
                    sp.wait_ge(result_ready, 2 * (t + 1))
                    sp.dma_start(out_rows[t], result[:, c, :]).then_inc(out_stored[c], 16)

                def step(r, c):
                    if live(at(r, c, 2)[0]):
                        load_window(*at(r, c, 2))
                    if live(at(r, c, 3)[0]):
                        store_x1(*at(r, c, 3))
                    if live(at(r, c, 3)[0]) and live(at(r, c, 5)[0]):
                        load_attention(*at(r, c, 5))
                    if live(at(r, c, 2)[0]):
                        load_conv_bias(*at(r, c, 2))
                    if live(at(r, c, 1)[0]):
                        load_x1(*at(r, c, 1))
                    if live(at(r, c, 0)[0]):
                        store_result(*at(r, c, 0))

                sp.wait_ge(edges, 4)
                run_steps(sp, step, FIRST, LOOP, ENDS, LAST)
                for c in range(2):
                    sp.wait_ge(out_stored[c], 16 * (PAIRS // 2))

            @block.gpsimd
            def _(pool):
                for c in range(2):
                    nc.gpsimd.memset(win[0:P // 2, c, :, 0:1], 0.0).then_inc(edges, 1)
                    pool.wait_ge(edges, 2 * c + 1)
                    nc.gpsimd.memset(win[P // 2:P, c, :, NJ:NJ + 1], 0.0).then_inc(edges, 1)
                    pool.wait_ge(edges, 2 * c + 2)

                for p in range(PH):
                    nc.gpsimd.tensor_scalar(signs[:, p, :], late.kernel_u8[:, p, :], 2.0, -1.0,
                                            ALU.mult, ALU.add).then_inc(signed, 1)

                def window_low_part(t, r, c):
                    pool.wait_ge(win_high, t + 1)
                    nc.gpsimd.tensor_tensor(win_lo[:, c].rearrange("p b g j -> p (b g) j"), win[:, c],
                                            win_hi[:, c].rearrange("p b g j -> p (b g) j").bitcast(F32),
                                            ALU.subtract).then_inc(win_low, 1)

                def conv_low_part(t, r, c):
                    for b in range(2):
                        part = slice(4 * b, 4 * b + 4)
                        pool.wait_ge(conv_high, 2 * t + b + 1)
                        nc.gpsimd.tensor_tensor(conv_lo[:, c, :, part], conv[:, :, part],
                                                conv_hi[:, c, :, part].bitcast(F32), ALU.subtract).then_inc(conv_low, 1)

                def step(r, c):
                    if live(at(r, c, 2)[0]):
                        window_low_part(*at(r, c, 2))
                    if live(at(r, c, 1)[0]):
                        conv_low_part(*at(r, c, 1))

                run_steps(pool, step, FIRST, LOOP, ENDS, LAST)

            @block.scalar
            def _(act):
                def window_high_part(t, r, c):
                    act.wait_ge(win_in[c], 16 * PH * (r + 1))
                    if live(t - 2):
                        act.wait_ge(conv_acc, 2 * (t - 1))
                    nc.scalar.activation(win_hi[:, c].rearrange("p b g j -> p (b g) j"), win[:, c],
                                         ACT.Copy).then_inc(win_high, 1)

                def conv_high_part(t, r, c):
                    if live(t - 2):
                        act.wait_ge(ffn_acc, 2 * (t - 1))
                    for b in range(2):
                        part = slice(4 * b, 4 * b + 4)
                        act.wait_ge(conv_added, 2 * t + b + 1)
                        nc.scalar.activation(conv_hi[:, c, :, part], conv[:, :, part], ACT.Copy).then_inc(conv_high, 1)

                def values_high_part(t, r, c):
                    if live(t - 2):
                        act.wait_ge(attn_in[c], 32 * r)
                        act.wait_ge(out_acc, 2 * (t - 1))
                    nc.scalar.activation(vals_hi[:, c], vals[:, c], ACT.Copy).then_inc(vals_high, 1)

                def step(r, c):
                    if live(at(r, c, 4)[0]):
                        values_high_part(*at(r, c, 4))
                    if live(at(r, c, 2)[0]):
                        window_high_part(*at(r, c, 2))
                    if live(at(r, c, 1)[0]):
                        conv_high_part(*at(r, c, 1))

                run_steps(act, step, FIRST, LOOP, ENDS, LAST)

            @block.vector
            def _(dve):
                def values_low_part(t, r, c):
                    dve.wait_ge(vals_high, t + 1)
                    nc.vector.tensor_tensor(vals_lo[:, c], vals[:, c], vals_hi[:, c].bitcast(F32),
                                            ALU.subtract).then_inc(vals_low, 1)
                    nc.vector.tensor_tensor(x_sb[:, c, :], x_sb[:, c, :], late.bo[:, :], ALU.add).then_inc(x_biased, 1)

                def add_x(t, r, c):
                    dve.wait_ge(x_biased, t + 1)
                    if live(t - 2):
                        dve.wait_ge(x1_stored[c], 16 * r)
                    x_phases = x_sb[:, c, :].rearrange("p (j q) -> p q j", q=PH)
                    for b in range(2):
                        part = slice(H4 * b, H4 * b + H4)
                        dve.wait_ge(out_acc, 2 * t + b + 1)
                        nc.vector.tensor_tensor(x1[:, c, part, :], out_ps[b][:, :].rearrange("p (q j) -> p q j", j=NJ),
                                                x_phases[:, part, :], ALU.add).then_inc(x1_ready, 1)

                def turn_conv(t, r, c):
                    if live(t - 1):
                        dve.wait_ge(conv_added, 2 * t)
                    for half in range(2):
                        dve.wait_ge(conv_acc, 2 * t + half + 1)
                        sums = conv_ps[half][:, :].rearrange("p (g b j) -> p b g j", g=2, b=2)
                        for i in range(P // TURN):
                            for j in range(P // TURN):
                                here, there = slice(TURN * i, TURN * (i + 1)), slice(TURN * j, TURN * (j + 1))
                                last = nc.vector.transpose(conv_sum[there, :, 2 * half:2 * half + 2, here], sums[here, :, :, there])
                        last.then_inc(conv_turned, 1)

                def add_conv_bias(t, r, c):
                    dve.wait_ge(convb_in[c], 16 * (r + 1))
                    dve.wait_ge(conv_turned, 2 * (t + 1))
                    for b in range(2):
                        part = slice(4 * b, 4 * b + 4)
                        if live(t - 1):
                            dve.wait_ge(conv_low, 2 * t + b - 1)
                        nc.vector.tensor_tensor(conv[:, :, part].rearrange("p q g o -> p g q o"),
                                                conv_sum[:, b, :, :].rearrange("p g (q o) -> p g q o", q=PH),
                                                convb_sb[:, c, part, :].unsqueeze(2).to_broadcast([P, 4, PH, GC]),
                                                ALU.add).then_inc(conv_added, 1)

                def finish(t, r, c):
                    dve.wait_ge(x1_in[c], 16 * (r + 1))
                    if live(t - 2):
                        dve.wait_ge(out_stored[c], 16 * r)
                    for b in range(2):
                        cols = slice(b * BANK, (b + 1) * BANK)
                        dve.wait_ge(ffn_acc, 2 * t + b + 1)
                        nc.vector.scalar_tensor_tensor(
                            out=result[:, c, cols].rearrange("p (j q) -> p j q", q=PH),
                            in0=ffn_ps[b][:, :].rearrange("p (j q) -> p j q", q=PH), scalar=late.scale[:, 0:1],
                            in1=x1_res[:, c, :, b * (NJ // 2):(b + 1) * (NJ // 2)].rearrange("p q j -> p j q"),
                            op0=ALU.mult, op1=ALU.add).then_inc(result_ready, 1)

                def step(r, c):
                    if live(at(r, c, 4)[0]):
                        values_low_part(*at(r, c, 4))
                    if live(at(r, c, 3)[0]):
                        add_x(*at(r, c, 3))
                    if live(at(r, c, 1)[0]):
                        turn_conv(*at(r, c, 1))
                        add_conv_bias(*at(r, c, 1))
                    if live(at(r, c, 0)[0]):
                        finish(*at(r, c, 0))

                run_steps(dve, step, FIRST, LOOP, ENDS, LAST)

            @block.tensor
            def _(pe):
                def project(t, r, c):
                    pe.wait_ge(vals_low, t + 1)
                    for b in range(2):
                        if live(t - 1):
                            pe.wait_ge(x1_ready, 2 * t + b - 1)
                        n = 0
                        for a in range(HP):
                            for v, w in ((vals_hi, wo_hi), (vals_hi, wo_lo), (vals_lo, wo_hi)):
                                last = pe.matmul(out_ps[b][:, :], v[:, c, a, :], w[:, a, b * BANK:(b + 1) * BANK],
                                                 start=(n == 0), stop=(n == 3 * HP - 1))
                                n += 1
                        last.then_inc(out_acc, 1)

                def convolve(t, r, c):
                    pe.wait_ge(win_low, t + 1)
                    for g in range(GROUPS):
                        if g % 2 == 0 and live(t - 1):
                            pe.wait_ge(conv_turned, 2 * t + g // 2 - 1)
                        n = 0
                        for d in range(2):
                            for band, w in ((bands_hi, win_hi), (bands_hi, win_lo), (bands_lo, win_hi)):
                                last = pe.matmul(conv_ps[g // 2][:, (g % 2) * 2 * NJ:(g % 2 + 1) * 2 * NJ], band[:, d, g, :],
                                                 w[:, c, :, g, d:d + NJ], start=(n == 0), stop=(n == 5))
                                n += 1
                        if g % 2 == 1:
                            last.then_inc(conv_acc, 1)

                def feed(t, r, c):
                    if isinstance(t, int) and t == 0:
                        pe.wait_ge(signed, PH)
                    pe.wait_ge(conv_low, 2 * (t + 1))
                    for b in range(2):
                        if live(t - 1):
                            pe.wait_ge(result_ready, 2 * t + b - 1)
                        n = 0
                        for p in range(PH):
                            for m in (conv_hi, conv_lo):
                                last = pe.matmul(ffn_ps[b][:, :], m[:, c, p].rearrange("p g o -> p (g o)"), signs[:, p, b * BANK:(b + 1) * BANK],
                                                 start=(n == 0), stop=(n == 2 * PH - 1))
                                n += 1
                        last.then_inc(ffn_acc, 1)

                def step(r, c):
                    if live(at(r, c, 3)[0]):
                        project(*at(r, c, 3))
                    if live(at(r, c, 1)[0]):
                        convolve(*at(r, c, 1))
                    if live(at(r, c, 0)[0]):
                        feed(*at(r, c, 0))

                run_steps(pe, step, FIRST, LOOP, ENDS, LAST)


_INS = ['x', 'cond_128', 'fside_S_0', 'L0_cond_W0', 'L0_cond_b0', 'L0_cond_W1', 'L0_cond_b1', 'L0_cond_W2',
        'L0_cond_b2', 'L0_cond_weight', 'L0_cond_bias_k', 'L0_attn_w_qkv', 'L0_attn_b_qkv', 'L0_attn_w_o',
        'L0_attn_b_o', 'L0_cond2_weight', 'L0_cond2_c_weight', 'L0_ffn_kernel', 'L0_ffn_scale']


def kernel(**inputs):
    import numpy as _np
    import concourse.bacc as _bacc
    from concourse import mybir as _mybir
    from concourse.bass_utils import run_bass_kernel_spmd as _run

    nc = _bacc.Bacc("TRN2", target_bir_lowering=False, num_devices=1)
    arrays, args = {}, []
    for name in _INS:
        a = _np.ascontiguousarray(inputs[name])
        if name == 'L0_ffn_scale':
            a = a.reshape(1, 1)
        arrays[f"in_{name}_dram"] = a
        args.append(nc.dram_tensor(f"in_{name}_dram", a.shape, _mybir.dt.from_np(a.dtype), kind="ExternalInput").ap())
    args.append(nc.dram_tensor("out_0_dram", (BATCH, SEQ, HID), F32, kind="ExternalOutput").ap())
    build(nc, *args)
    r = _run(nc, [arrays], core_ids=[0])
    return r.results[0]["out_0_dram"]
```
